# Optimizing a Trainium2 kernel written in Bass

```python
import numpy as np
import jax
import jax.numpy as jnp

def _softmax(x, axis=-1):
    return jax.nn.softmax(x, axis=axis)

def _gelu(x):
    return jax.nn.gelu(x, approximate=True)

def _silu(x):
    return jax.nn.silu(x)

def _sigmoid(x):
    return jax.nn.sigmoid(x)

def _layernorm(x, axis=-1, eps=1e-05):
    m = jnp.mean(x, axis=axis, keepdims=True)
    v = jnp.var(x, axis=axis, keepdims=True)
    return (x - m) / jnp.sqrt(v + eps)

def _scatter_add(tgt, idx, src, axis=0):
    return tgt.at[idx].add(src)

def _segment_sum(src, seg, n):
    return jax.ops.segment_sum(src, seg, n)
kernel_name = 'mk_seq_preln_d1_jaxref_r4_0ed402'

def setup_inputs(seed: int=0):
    np.random.seed(seed)
    _w = jnp.asarray

    def _L0_attn_setup():
        import jax, jax.numpy as jnp
        import numpy as np
        B, L, E, H = (2, 512, 256, 16)
        HD = E // H
        THETA = 10000.0

        def _rope_tables(seq_len, dim, dtype):
            inv_freq = 1.0 / THETA ** (jnp.arange(0, dim, 2, dtype=jnp.float32) / dim)
            freqs = jnp.arange(seq_len, dtype=jnp.float32)[:, None] * inv_freq[None, :]
            freqs = jnp.repeat(freqs, 2, axis=-1)
            return (jnp.cos(freqs).astype(dtype), jnp.sin(freqs).astype(dtype))

        def _rotate_half(x):
            x2 = x.reshape(*x.shape[:-1], -1, 2)
            x2 = jnp.stack([-x2[..., 1], x2[..., 0]], axis=-1)
            return x2.reshape(x.shape)

        def _apply_rope(x, cos, sin):
            return x * cos[None, None] + _rotate_half(x) * sin[None, None]
        key = jax.random.key(seed)
        ks = jax.random.split(key, 9)
        s = 1.0 / np.sqrt(E)
        return {'x': jax.random.normal(ks[0], (B, L, E), jnp.float32), 'Wq': jax.random.normal(ks[1], (E, E), jnp.float32) * s, 'bq': jax.random.normal(ks[2], (E,), jnp.float32) * 0.01, 'Wk': jax.random.normal(ks[3], (E, E), jnp.float32) * s, 'bk': jax.random.normal(ks[4], (E,), jnp.float32) * 0.01, 'Wv': jax.random.normal(ks[5], (E, E), jnp.float32) * s, 'bv': jax.random.normal(ks[6], (E,), jnp.float32) * 0.01, 'Wo': jax.random.normal(ks[7], (E, E), jnp.float32) * s, 'bo': jax.random.normal(ks[8], (E,), jnp.float32) * 0.01}
    _L0_attn_in = _L0_attn_setup()

    def _L0_ffn_setup():
        import jax, jax.numpy as jnp
        import numpy as np
        B, S, H, I, E, K = (4, 512, 256, 256, 8, 2)
        LIMIT = 7.0
        ALPHA = 1.702
        EPS = 1e-05
        key = jax.random.key(seed)
        ks = jax.random.split(key, 5)
        x = jax.random.normal(ks[0], (B, S, H), dtype=jnp.float32)
        norm_weight = jnp.ones((H,), dtype=jnp.float32)
        gate_weight = (jax.random.normal(ks[1], (E, H), dtype=jnp.float32) / np.sqrt(H)).astype(jnp.bfloat16)
        gate_bias = jnp.zeros((E,), dtype=jnp.bfloat16)
        mlp1_weight = (jax.random.normal(ks[2], (E, 2 * I, H), dtype=jnp.float32) / np.sqrt(H)).astype(jnp.bfloat16)
        mlp1_bias = jnp.zeros((E, 2 * I), dtype=jnp.bfloat16)
        mlp2_weight = (jax.random.normal(ks[3], (E, H, I), dtype=jnp.float32) / np.sqrt(I)).astype(jnp.bfloat16)
        mlp2_bias = jnp.zeros((E, H), dtype=jnp.bfloat16)
        return {'x': x, 'norm_weight': norm_weight, 'gate_weight': gate_weight, 'gate_bias': gate_bias, 'mlp1_weight': mlp1_weight, 'mlp1_bias': mlp1_bias, 'mlp2_weight': mlp2_weight, 'mlp2_bias': mlp2_bias}
    _L0_ffn_in = _L0_ffn_setup()
    _d = {'L0_attn_x': _L0_attn_in['x'], 'L0_attn_Wq': _L0_attn_in['Wq'], 'L0_attn_bq': _L0_attn_in['bq'], 'L0_attn_Wk': _L0_attn_in['Wk'], 'L0_attn_bk': _L0_attn_in['bk'], 'L0_attn_Wv': _L0_attn_in['Wv'], 'L0_attn_bv': _L0_attn_in['bv'], 'L0_attn_Wo': _L0_attn_in['Wo'], 'L0_attn_bo': _L0_attn_in['bo'], 'L0_ffn_norm_weight': _L0_ffn_in['norm_weight'], 'L0_ffn_gate_weight': _L0_ffn_in['gate_weight'], 'L0_ffn_gate_bias': _L0_ffn_in['gate_bias'], 'L0_ffn_mlp1_weight': _L0_ffn_in['mlp1_weight'], 'L0_ffn_mlp1_bias': _L0_ffn_in['mlp1_bias'], 'L0_ffn_mlp2_weight': _L0_ffn_in['mlp2_weight'], 'L0_ffn_mlp2_bias': _L0_ffn_in['mlp2_bias']}
    _x0 = _d['L0_attn_x']
    _d['L0_attn_x'] = jax.random.normal(jax.random.fold_in(jax.random.key(seed), 1), (4, 1024, 256), dtype=_x0.dtype)
    del _x0
    return _d

def reference(L0_attn_x, L0_attn_Wq, L0_attn_bq, L0_attn_Wk, L0_attn_bk, L0_attn_Wv, L0_attn_bv, L0_attn_Wo, L0_attn_bo, L0_ffn_norm_weight, L0_ffn_gate_weight, L0_ffn_gate_bias, L0_ffn_mlp1_weight, L0_ffn_mlp1_bias, L0_ffn_mlp2_weight, L0_ffn_mlp2_bias):

    def _L0_attn_ref(x, Wq, bq, Wk, bk, Wv, bv, Wo, bo):
        import jax, jax.numpy as jnp
        import numpy as np
        B, L, E, H = (2, 512, 256, 16)
        HD = E // H
        THETA = 10000.0

        def _rope_tables(seq_len, dim, dtype):
            inv_freq = 1.0 / THETA ** (jnp.arange(0, dim, 2, dtype=jnp.float32) / dim)
            freqs = jnp.arange(seq_len, dtype=jnp.float32)[:, None] * inv_freq[None, :]
            freqs = jnp.repeat(freqs, 2, axis=-1)
            return (jnp.cos(freqs).astype(dtype), jnp.sin(freqs).astype(dtype))

        def _rotate_half(x):
            x2 = x.reshape(*x.shape[:-1], -1, 2)
            x2 = jnp.stack([-x2[..., 1], x2[..., 0]], axis=-1)
            return x2.reshape(x.shape)

        def _apply_rope(x, cos, sin):
            return x * cos[None, None] + _rotate_half(x) * sin[None, None]
        b, l, e = x.shape
        q = (x @ Wq.T + bq).reshape(b, l, H, HD).transpose(0, 2, 1, 3)
        k = (x @ Wk.T + bk).reshape(b, l, H, HD).transpose(0, 2, 1, 3)
        v = (x @ Wv.T + bv).reshape(b, l, H, HD).transpose(0, 2, 1, 3)
        cos, sin = _rope_tables(l, HD, x.dtype)
        q = _apply_rope(q, cos, sin)
        k = _apply_rope(k, cos, sin)
        scale = 1.0 / np.sqrt(HD)
        scores = jnp.einsum('bhsd,bhed->bhse', q, k) * scale
        attn = jax.nn.softmax(scores, axis=-1)
        out = jnp.einsum('bhse,bhed->bhsd', attn, v)
        out = out.transpose(0, 2, 1, 3).reshape(b, l, e)
        return out @ Wo.T + bo

    def _L0_ffn_ref(x, norm_weight, gate_weight, gate_bias, mlp1_weight, mlp1_bias, mlp2_weight, mlp2_bias):
        import jax, jax.numpy as jnp
        import numpy as np
        B, S, H, I, E, K = (4, 512, 256, 256, 8, 2)
        LIMIT = 7.0
        ALPHA = 1.702
        EPS = 1e-05
        xc = x.astype(jnp.bfloat16)
        xf = xc.astype(jnp.float32)
        rms = jnp.mean(xf * xf, axis=-1, keepdims=True)
        normed = (xf * jax.lax.rsqrt(rms + EPS) * norm_weight).astype(jnp.bfloat16)
        nf = normed.astype(jnp.float32)
        logits = (jnp.einsum('bsh,eh->bse', nf, gate_weight.astype(jnp.float32)) + gate_bias.astype(jnp.float32)).astype(jnp.bfloat16).astype(jnp.float32)
        scores, idx = jax.lax.top_k(logits, K)
        w = jax.nn.softmax(scores, axis=-1)
        combine = jnp.sum(jax.nn.one_hot(idx, E, dtype=jnp.float32) * w[..., None], axis=-2)
        p1 = jnp.einsum('bsh,eoh->bseo', nf, mlp1_weight.astype(jnp.float32)) + mlp1_bias.astype(jnp.float32)
        g = jnp.minimum(p1[..., 0::2], LIMIT)
        lin = jnp.clip(p1[..., 1::2], -LIMIT, LIMIT)
        act = g * jax.nn.sigmoid(ALPHA * g) * (lin + 1.0)
        p2 = jnp.einsum('bsei,ehi->bseh', act, mlp2_weight.astype(jnp.float32)) + mlp2_bias.astype(jnp.float32)
        combined = jnp.einsum('bseh,bse->bsh', p2, combine)
        out = (xc + combined.astype(jnp.bfloat16)).astype(x.dtype)
        return out
    x = L0_attn_x
    x = x + _L0_attn_ref(_layernorm(x, axis=-1), L0_attn_Wq, L0_attn_bq, L0_attn_Wk, L0_attn_bk, L0_attn_Wv, L0_attn_bv, L0_attn_Wo, L0_attn_bo)
    x = x + _L0_ffn_ref(_layernorm(x, axis=-1), L0_ffn_norm_weight, L0_ffn_gate_weight, L0_ffn_gate_bias, L0_ffn_mlp1_weight, L0_ffn_mlp1_bias, L0_ffn_mlp2_weight, L0_ffn_mlp2_bias)
    return x

_drawn_inputs = setup_inputs


def setup_inputs(seed=0):
    import zlib

    import numpy as np

    out = dict(_drawn_inputs(seed))
    spreads = {'L0_ffn_norm_weight': (1.0, 0.2)}
    factors = {'L0_attn_bq': 24.868, 'L0_attn_bk': 25.462, 'L0_attn_bo': 2.712}
    for name, (base, spread) in spreads.items():
        noise = np.random.default_rng([zlib.crc32(name.encode()), seed]).standard_normal(out[name].shape)
        drawn = base * np.exp(spread * noise) if base else spread * noise
        out[name] = jnp.asarray(drawn.astype(out[name].dtype))
    for name, factor in factors.items():
        out[name] = (out[name] * factor).astype(out[name].dtype)
    return out
```

```python
from contextlib import ExitStack

import concourse.bass as bass
from concourse import mybir

FP32 = mybir.dt.float32
FP32R = mybir.dt.float32r
BF16 = mybir.dt.bfloat16
INT32 = mybir.dt.int32
ALU = mybir.AluOpType
ACT = mybir.ActivationFunctionType
AX_X = mybir.AxisListType.X

P = 128
B, L, E = 4, 1024, 256
H, HD = 16, 16
NE, TOPK, FI = 8, 2, 256
LIMIT, ALPHA, EPS = 7.0, 1.702, 1e-5
CT = E // P
TT = L // P
HG = 4
NG = H // HG
KT = L // P
STEPS = NG * KT
NCH = L // 512
SROWS = 6 * HD
MROWS = 2
VW = HD + 1
SCALE = HD ** -0.5
SAFE_SCORE = 60.0
Q_PARTS = (0, 0, 0, 1, 1, 2)
K_PARTS = (0, 1, 2, 0, 1, 0)


def block_kernel(nc, x, wqk, bqk, wv, bv, wo, nw, gate, gate_b, w1, b1, w2, b2, rope, ident_in, heads_in, rank_in,
                 out, safe_score=SAFE_SCORE):
    ctx = ExitStack()
    with ctx:
        def sb(name, shape, dt):
            return ctx.enter_context(nc.sbuf_tensor(name, shape, dt))

        def ps(name, shape, dt):
            return ctx.enter_context(nc.psum_tensor(name, shape, dt))

        def sem(name):
            return ctx.enter_context(nc.semaphore(name))

        def scratch(name, shape, dt):
            return nc.dram_tensor(name, shape, dt, kind="Internal").ap()

        qk_scr = scratch("qk_scr", (B, 2, 3, E, L), BF16)
        m_scr = scratch("m_scr", (B, MROWS, H, L), BF16)
        sum_scr = scratch("sum_scr", (B * NG, HG, L), FP32)
        rec_scr = scratch("rec_scr", (B * NG, HG, L), FP32)

        wqk_sb = sb("wqk_sb", [P, CT, 2 * E], FP32)
        bqk_sb = sb("bqk_sb", [P, 4], FP32)
        wv_sb = sb("wv_sb", [P, CT, E], FP32)
        bv_sb = sb("bv_sb", [P, E], FP32)
        wo_sb = sb("wo_sb", [P, NG, E], FP32)
        nw_sb = sb("nw_sb", [P, E], FP32)
        gate_sb = sb("gate_sb", [P, CT, NE], BF16)
        gate_b_sb = sb("gate_b_sb", [P, NE], BF16)
        b1_sb = sb("b1_sb", [P, NE, 2, CT], BF16)
        b1f = sb("b1f", [P, NE, 2, CT], FP32)
        b2_sb = sb("b2_sb", [NE, E], BF16)
        b2f = sb("b2f", [NE, E], FP32)
        cos_sb = sb("cos_sb", [P, L], FP32)
        sin_sb = sb("sin_sb", [P, L], FP32)
        ident = sb("ident", [P, P], FP32)
        identb = sb("identb", [P, P], BF16)
        same_head = sb("same_head", [P, P], BF16)
        rank = sb("rank", [P, NE], FP32)
        half_pow = sb("half_pow", [P, TT], FP32)

        X = sb("X", [P, TT, E], FP32)
        X1 = sb("X1", [P, TT, E], FP32)
        xnT = sb("xnT", [P, CT, L], FP32)
        V = sb("V", [P, KT, H, VW], FP32)
        Qs = sb("Qs", [P, 2, HG, L], BF16)
        Ks = sb("Ks", [P, 2, HG, L], BF16)
        probs = sb("probs", [P, 2, HG, L], FP32)
        O = sb("O", [P, NG, L], FP32)
        rec_b = sb("rec_b", [P, L], FP32)
        sums_c = sb("sums_c", [P, 32], FP32)
        rec_c = sb("rec_c", [P, 32], FP32)
        xc = sb("xc", [P, TT, E], BF16)
        nfT = sb("nfT", [P, CT, L], BF16)
        acc = sb("acc", [P, TT, E], FP32)
        W1 = sb("W1", [P, 2, CT, 2 * FI], BF16)
        W2b = sb("W2b", [P, 2, CT, E], BF16)
        W2 = sb("W2", [P, 2, CT, E], FP32R)
        act_hi = sb("act_hi", [P, 2, CT, 512], FP32R)
        act_lo = sb("act_lo", [P, 2, CT, 512], FP32R)
        ffn = sb("ffn", [P, 8 * 512], FP32)
        g_sb = [ffn[:, i * 512:(i + 1) * 512] for i in (0, 1)]
        l_sb = [ffn[:, i * 512:(i + 1) * 512] for i in (2, 3)]
        th_sb = [ffn[:, i * 512:(i + 1) * 512] for i in (4, 5)]
        act_sb = [ffn[:, i * 512:(i + 1) * 512] for i in (6, 7)]
        Mt = sb("Mt", [H, MROWS, L], BF16)
        mx = sb("mx", [P, TT, H], FP32)

        xn = probs[:, 0, 0:2, :].rearrange("p a (t c) -> p (a t) c", c=E)
        qb = [probs[:, 0, 2, :], probs[:, 0, 3, :]]
        sw = [probs[:, 1, 0, :], probs[:, 1, 1, :]]
        rot = [probs[:, 1, 2, :], probs[:, 1, 3, :]]
        scr16 = ffn[:, :].bitcast(BF16)
        parts = [scr16[:, i * 3 * L:(i + 1) * 3 * L].rearrange("p (a t) -> p a t", a=3) for i in (0, 1)]
        sq = scr16[:, 6 * L:7 * L]
        nf = scr16[:, 0:2 * L].rearrange("p (t c) -> p t c", c=E)

        st1 = sb("st1", [P, TT, 6], FP32)
        mv1 = sb("mv1", [P, TT, 2], FP32)
        var1 = sb("var1", [P, TT], FP32)
        rstd1 = sb("rstd1", [P, TT], FP32)
        st2 = sb("st2", [P, TT, 6], FP32)
        mv2 = sb("mv2", [P, TT, 2], FP32)
        var2 = sb("var2", [P, TT], FP32)
        rstd2 = sb("rstd2", [P, TT], FP32)
        sqs = sb("sqs", [P, E], FP32)
        ss = sb("ss", [P, TT], FP32)
        ms = sb("ms", [P, TT], FP32)
        rrms = sb("rrms", [P, TT], FP32)
        nsq = sb("nsq", [P, 2, 4], FP32)
        nsq2 = sb("nsq2", [P, 2], FP32)
        nsqa = sb("nsqa", [P, 2], FP32)
        bound = sb("bound", [P, 1], FP32)
        exact_flag = sb("exact_flag", [P, B], INT32)
        lgb = sb("lgb", [P, TT, NE], BF16)
        lgt = sb("lgt", [P, TT, NE], FP32)
        top1 = sb("top1", [P, TT], FP32)
        top2 = sb("top2", [P, TT], FP32)
        pick = sb("pick", [P, TT, NE], FP32)
        pickm = sb("pickm", [P, TT], FP32)
        oh1 = sb("oh1", [P, TT, NE], FP32)
        oh2 = sb("oh2", [P, TT, NE], FP32)
        lg2 = sb("lg2", [P, TT, NE], FP32)
        dtop = sb("dtop", [P, TT], FP32)
        etop = sb("etop", [P, TT], FP32)
        w_1 = sb("w_1", [P, TT], FP32)
        w_2 = sb("w_2", [P, TT], FP32)
        comb = sb("comb", [P, TT, NE], FP32)
        combh = sb("combh", [P, TT, NE], FP32)
        combT = ffn[0:NE, L:2 * L]

        S = ps("S", [P, 2, L], FP32)
        OP = ps("OP", [P, L], FP32)
        A = ps("A", [P, 512], FP32)
        BB = ps("BB", [P, 512], FP32)

        c_ld = sem("c_ld")
        passed = sem("passed")
        c_set = sem("c_set")
        x_ld = sem("x_ld")
        stat1, aggr1, var1_s, rstd1_s, xn_s = (sem(n) for n in ("stat1", "aggr1", "var1_s", "rstd1_s", "xn_s"))
        xt_mm, xnT_a, xnT_v = sem("xt_mm"), sem("xnT_a"), sem("xnT_v")
        qk_mm, qk_b, qk_sw, qk_sin, qk_cos, qk_rot = (sem(n) for n in ("qk_mm", "qk_b", "qk_sw", "qk_sin", "qk_cos", "qk_rot"))
        qk_p1, qk_sq, qk_r1, qk_p2, qk_p3 = (sem(n) for n in ("qk_p1", "qk_sq", "qk_r1", "qk_p2", "qk_p3"))
        scr_w = [sem("scr_w0"), sem("scr_w1")]
        nrm_mm, nrm_red, nsq_s, nsqa_s, bound_s, flag_s = (sem(n) for n in ("nrm_mm", "nrm_red", "nsq_s", "nsqa_s", "bound_s", "flag_s"))
        v_mm, v_done = sem("v_mm"), sem("v_done")
        ex_ld = [sem("ex_ld0"), sem("ex_ld1")]
        ex_mm, ex_red, ex_t = sem("ex_mm"), sem("ex_red"), sem("ex_t")
        m_set, m_w = sem("m_set"), sem("m_w")
        st_ld = [sem("st_ld0"), sem("st_ld1")]
        s_done, exp_done, av_done = sem("s_done"), sem("exp_done"), sem("av_done")
        o_ev, sum_w, sum_r, rec_s, rec_w, rec_r, on_s = (sem(n) for n in ("o_ev", "sum_w", "sum_r", "rec_s", "rec_w", "rec_r", "on_s"))
        x1_ld, y_mm, x1_s = sem("x1_ld"), sem("y_mm"), sem("x1_s")
        stat2, aggr2, var2_s, rstd2_s, xc_s = (sem(n) for n in ("stat2", "aggr2", "var2_s", "rstd2_s", "xc_s"))
        ss_s, ms_s, rrms_s, nf_s, nft_mm, nfT_a, nfT_v = (sem(n) for n in ("ss_s", "ms_s", "rrms_s", "nf_s", "nft_mm", "nfT_a", "nfT_v"))
        lg_mm, gating, dtop_s, etop_s, comb_s, ct_mm, combT_s, b2_mm, acc_s = (
            sem(n) for n in ("lg_mm", "gating", "dtop_s", "etop_s", "comb_s", "ct_mm", "combT_s", "b2_mm", "acc_s"))
        w1_ld = [sem("w1_ld0"), sem("w1_ld1")]
        w2_ld = [sem("w2_ld0"), sem("w2_ld1")]
        w2_s = sem("w2_s")
        m1_mm, g_s, l_s, th_s, t1_s, act_s, hi_s, lo_s, m2_mm, m2_ev = (
            sem(n) for n in ("m1_mm", "g_s", "l_s", "th_s", "t1_s", "act_s", "hi_s", "lo_s", "m2_mm", "m2_ev"))
        cb_s, fo_s, x2_s, out_w = sem("cb_s"), sem("fo_s"), sem("x2_s"), sem("out_w")

        CONST_LOADS = 15
        N_CONST_SET = 9
        M2 = STEPS

        x_v = x.rearrange("b (t p) c -> b p t c", p=P)
        out_v = out.rearrange("b (t p) c -> b p t c", p=P)

        block = ctx.enter_context(nc.Block())

        def wait_apart(engine, *waits):
            for signal, value in waits:
                engine.wait_ge(signal, value)
                engine.sem_inc(passed, 1)

        @block.sync
        def _(sp):
            for dst, src in (
                (wqk_sb[:, :, :], wqk.rearrange("(c p) n -> p c n", p=P)), (bqk_sb[:, :], bqk),
                (wv_sb[:, :, :], wv.rearrange("(c p) n -> p c n", p=P)), (bv_sb[:, :], bv[None, :].to_broadcast([P, E])),
                (wo_sb[:, :, :], wo.rearrange("g p n -> p g n")), (nw_sb[:, :], nw[None, :].to_broadcast([P, E])),
                (gate_sb[:, :, :], gate.rearrange("(c p) n -> p c n", p=P)),
                (gate_b_sb[:, :], gate_b[None, :].to_broadcast([P, NE])),
                (b1_sb[:, :, :, :], b1), (b2_sb[:, :], b2), (cos_sb[:, :], rope[0]), (sin_sb[:, :], rope[1]),
                (ident[:, :], ident_in), (rank[:, :], rank_in[None, :].to_broadcast([P, NE])),
            ):
                sp.dma_start(dst, src).then_inc(c_ld, 16)
            sp.dma_start(th_sb[0][:, 0:P], heads_in).then_inc(c_ld, 16)

            def load_x(b):
                sp.dma_start(X[:, :, :], x_v[b]).then_inc(x_ld, 16)

            def load_expert(fb, e):
                sp.dma_start(W1[:, e % 2, :, :], w1[e]).then_inc(w1_ld[e % 2], 16)
                sp.dma_start(W2b[:, e % 2, :, :], w2[e]).then_inc(w2_ld[e % 2], 16)

            def stack(b, g, slot, signal, shifts):
                for blk, (qp, kp) in enumerate(zip(Q_PARTS, K_PARTS)):
                    for t, dst, part in ((0, Qs, qp), (1, Ks, kp)):
                        src = qk_scr[b, t, part, HG * HD * g:HG * HD * (g + 1), :].rearrange("(j d) t -> d j t", d=HD)
                        sp.dma_start(dst[HD * blk:HD * (blk + 1), slot, :, :], src).then_inc(signal, 16)
                if shifts:
                    sp.dma_start(Qs[SROWS:SROWS + MROWS, slot, :, :], m_scr[b, :, HG * g:HG * (g + 1), :]).then_inc(signal, 16)

            def prep(b):
                for i in range(4):
                    sp.wait_ge(qk_p3, 4 * b + i + 1)
                    sp.dma_start(qk_scr[b, i // 2, :, P * (i % 2):P * (i % 2 + 1), :].rearrange("a p t -> p a t"),
                                 parts[i % 2]).then_inc(scr_w[i % 2], 16)

            def exact(b):
                wait_apart(sp, (scr_w[0], 32 * (b + 1)), (scr_w[1], 32 * (b + 1)), (flag_s, b + 1))
                flag = sp.value_load(exact_flag[0:1, bass.ds(b, 1)], min_val=0, max_val=1)
                with sp.If(flag > 0):
                    for g in range(NG):
                        if g >= 2:
                            sp.wait_ge(ex_mm, 128 * b + 32 * (g - 1))
                        stack(b, g, g % 2, ex_ld[g % 2], False)
                with sp.If(flag < 1):
                    sp.sem_inc(ex_ld[0], 384)
                    sp.sem_inc(ex_ld[1], 384)
                sp.wait_ge(m_set, 2 * (b + 1))
                sp.dma_start(m_scr[b].rearrange("r h t -> h r t"), Mt[:, :, :]).then_inc(m_w, 16)
                sp.wait_ge(m_w, 16 * (b + 1))
                stack(b, 0, 0, st_ld[0], True)
                stack(b, 1, 1, st_ld[1], True)

            def sums(b, g):
                G = NG * b + g
                sp.wait_ge(o_ev, G + 1)
                for j in range(HG):
                    sp.dma_start(sum_scr[G, j:j + 1, :], O[32 * j + HD:32 * j + HD + 1, g, :]).then_inc(sum_w, 16)
                sp.wait_ge(sum_w, 64 * (G + 1))
                sp.dma_start(sums_c[:, :], sum_scr[G].rearrange("h (j t) -> (h j) t", t=32)).then_inc(sum_r, 16)
                sp.wait_ge(rec_s, G + 1)
                sp.dma_start(rec_scr[G].rearrange("h (j t) -> (h j) t", t=32), rec_c[:, :]).then_inc(rec_w, 16)
                sp.wait_ge(rec_w, 16 * (G + 1))
                sp.wait_ge(on_s, G) if not (isinstance(G, int) and G == 0) else None
                for j in range(HG):
                    sp.dma_start(rec_b[32 * j:32 * (j + 1), :],
                                 rec_scr[G, j:j + 1, :].to_broadcast([32, L])).then_inc(rec_r, 16)

            def attention(b, fb):
                for s in range(STEPS):
                    g, kt = divmod(s, KT)
                    if fb is not None and s % 4 == 3 and s // 4 + 2 < NE:
                        e = s // 4
                        wait_apart(sp, (m1_mm, 64 * fb + 8 * (e + 1)))
                        sp.wait_ge(w2_s, NE * fb + e + 1)
                        load_expert(fb, e + 2)
                    if kt == KT - 1:
                        if g < 2:
                            sp.wait_ge(s_done, 128 * b + 32 * (g + 1))
                            stack(b, g + 2, g % 2, st_ld[g % 2], True)
                        sums(b, g)

            def experts_alone(fb):
                for e in range(NE - 2):
                    sp.wait_ge(m1_mm, 64 * fb + 8 * (e + 1))
                    sp.wait_ge(w2_s, NE * fb + e + 1)
                    load_expert(fb, e + 2)

            def store(fb):
                sp.wait_ge(x2_s, 2 * (fb + 1))
                sp.dma_start(out_v[fb], acc[:, :, :]).then_inc(out_w, 16)

            def load_x1(b):
                sp.dma_start(X1[:, :, :], x_v[b]).then_inc(x1_ld, 16)

            load_x(0)
            prep(0)
            exact(0)
            sp.wait_ge(xn_s, TT)
            load_x(1)
            load_x1(0)
            load_expert(0, 0)
            load_expert(0, 1)
            attention(0, None)
            with sp.Fori(1, B) as b:
                prep(b)
                exact(b)
                sp.wait_ge(xn_s, TT * (b + 1))
                sp.dma_start(X[:, :, :], x_v[bass.ds((b + 1) % B, 1)].rearrange("o p t c -> (o p) t c")).then_inc(x_ld, 16)
                attention(b, b - 1)
                store(b - 1)
                wait_apart(sp, (x2_s, 2 * b), (out_w, 16 * b))
                load_x1(b)
                load_expert(b, 0)
                load_expert(b, 1)
            experts_alone(B - 1)
            store(B - 1)
            sp.wait_ge(out_w, 16 * B)
            sp.wait_ge(x_ld, 16 * (B + 1))

        @block.tensor
        def _(pe):
            mm = nc.tensor.matmul

            def prep(b):
                if not isinstance(b, int):
                    pe.wait_ge(exp_done, 128 * b)
                for c in range(CT):
                    for t in range(TT):
                        if c == 0:
                            pe.wait_ge(xn_s, TT * b + t + 1)
                        last = nc.tensor.transpose(S[:, c, P * t:P * (t + 1)], xn[:, t, P * c:P * (c + 1)], ident[:, :])
                    last.then_inc(xt_mm, 1)
                pe.wait_ge(xnT_a, b + 1)
                pe.wait_ge(xnT_v, b + 1)
                for i in range(4):
                    if i >= 2:
                        pe.wait_ge(qk_b, 4 * b + i - 1)
                    for n in range(NCH):
                        for c in range(CT):
                            last = mm(S[:, i % 2, 512 * n:512 * (n + 1)], wqk_sb[:, c, P * i:P * (i + 1)],
                                      xnT[:, c, 512 * n:512 * (n + 1)], start=c == 0, stop=c == CT - 1)
                    last.then_inc(qk_mm, 1)
                    if i >= 1:
                        norms(b, i - 1)
                for hf in range(2):
                    pe.wait_ge(qk_b, 4 * b + 3 + hf)
                    for t in range(4):
                        for c in range(CT):
                            last = mm(S[:, hf, E * t:E * (t + 1)], xnT[:, c, P * (4 * hf + t):P * (4 * hf + t + 1)],
                                      wv_sb[:, c, :], start=c == 0, stop=c == CT - 1)
                    last.then_inc(v_mm, 1)
                    if hf == 0:
                        norms(b, 3)

            def norms(b, i):
                pe.wait_ge(qk_sq, 4 * b + i + 1)
                if i >= 1:
                    pe.wait_ge(nrm_red, 8 * b + 2 * i)
                mm(A[:, :], same_head[:, :], sq[:, 0:512], start=True, stop=True)
                mm(BB[:, :], same_head[:, :], sq[:, 512:1024], start=True, stop=True).then_inc(nrm_mm, 1)

            def exact(b):
                wait_apart(pe, (v_done, 2 * (b + 1)), (flag_s, b + 1))
                flag = pe.value_load(exact_flag[0:1, bass.ds(b, 1)], min_val=0, max_val=1)
                with pe.If(flag > 0):
                    for g in range(NG):
                        pe.wait_ge(ex_ld[g % 2], 384 * b + 192 * (g // 2 + 1))
                        for j in range(HG):
                            for t in range(TT):
                                i = 32 * g + 8 * j + t
                                if i >= 2:
                                    pe.wait_ge(ex_red, 128 * b + i - 1)
                                for n in range(NCH):
                                    last = mm(S[:, i % 2, 512 * n:512 * (n + 1)],
                                              Qs[0:SROWS, g % 2, j, P * t:P * (t + 1)],
                                              Ks[0:SROWS, g % 2, j, 512 * n:512 * (n + 1)], start=True, stop=True)
                                last.then_inc(ex_mm, 1)
                    pe.wait_ge(ex_red, 128 * (b + 1))
                    for t in range(TT):
                        last = nc.tensor.transpose(S[0:H, 0, P * t:P * (t + 1)], mx[:, t, :], ident[:, :])
                    last.then_inc(ex_t, 1)
                with pe.If(flag < 1):
                    pe.sem_inc(ex_mm, 128)
                    pe.sem_inc(ex_t, 1)
                pe.wait_ge(m_set, 2 * (b + 1))

            def post(b):
                pe.wait_ge(on_s, NG * (b + 1))
                for hf in range(2):
                    for t in range(4):
                        tok = P * (4 * hf + t)
                        for g in range(NG):
                            last = mm(S[:, hf, E * t:E * (t + 1)], O[:, g, tok:tok + P], wo_sb[:, g, :],
                                      start=g == 0, stop=g == NG - 1)
                    last.then_inc(y_mm, 1)
                for c, bank in ((0, A), (1, BB)):
                    for t in range(TT):
                        if c == 0:
                            pe.wait_ge(nf_s, TT * b + t + 1)
                        last = nc.tensor.transpose(bank[:, :].bitcast(BF16)[:, P * t:P * (t + 1)],
                                                   nf[:, t, P * c:P * (c + 1)], identb[:, :])
                    last.then_inc(nft_mm, 1)
                pe.wait_ge(nfT_a, b + 1)
                pe.wait_ge(nfT_v, b + 1)
                for t in range(TT):
                    for c in range(CT):
                        last = mm(OP[:, NE * t:NE * (t + 1)], nfT[:, c, P * t:P * (t + 1)], gate_sb[:, c, :],
                                  start=c == 0, stop=c == CT - 1)
                last.then_inc(lg_mm, 1)
                pe.wait_ge(comb_s, 3 * (b + 1))
                for t in range(TT):
                    last = nc.tensor.transpose(OP[0:NE, P * t:P * (t + 1)], comb[:, t, :], ident[:, :])
                last.then_inc(ct_mm, 1)
                pe.wait_ge(combT_s, b + 1)
                for hf in range(2):
                    for t in range(4):
                        tok = P * (4 * hf + t)
                        last = mm(S[:, hf, E * t:E * (t + 1)], combT[:, tok:tok + P], b2f[:, :], start=True, stop=True)
                    last.then_inc(b2_mm, 1)

            def scores(b, s, j):
                g, kt = divmod(s, KT)
                if j == 0 and kt == 0:
                    pe.wait_ge(st_ld[g % 2], 416 * b + 208 * (g // 2 + 1))
                if 4 * s + j >= 2:
                    pe.wait_ge(exp_done, 128 * b + 4 * s + j - 1)
                elif not isinstance(b, int):
                    pe.wait_ge(acc_s, 2 * b - 1 + j)
                for n in range(NCH):
                    last = mm(S[:, j % 2, 512 * n:512 * (n + 1)], Ks[0:SROWS + MROWS, g % 2, j, P * kt:P * (kt + 1)],
                              Qs[0:SROWS + MROWS, g % 2, j, 512 * n:512 * (n + 1)], start=True, stop=True)
                last.then_inc(s_done, 1)

            def values(b, s, n):
                g, kt = divmod(s, KT)
                if n == 0:
                    pe.wait_ge(exp_done, 128 * b + 4 * (s + 1))
                    if kt == 0 and not (isinstance(b, int) and b == 0 and g == 0):
                        pe.wait_ge(o_ev, NG * b + g)
                for j in range(HG):
                    last = mm(OP[32 * j:32 * j + VW, 512 * n:512 * (n + 1)], V[:, kt, HG * g + j, :],
                              probs[:, s % 2, j, 512 * n:512 * (n + 1)], start=kt == 0, stop=kt == KT - 1)
                if n == NCH - 1:
                    last.then_inc(av_done, 1)

            def expert_up(fb, s):
                u, it = divmod(s, 2)
                e, n = divmod(u, NCH)
                if n == 0 and it == 0:
                    pe.wait_ge(w1_ld[e % 2], 16 * (4 * fb + e // 2 + 1))
                if s >= 3:
                    pe.wait_ge(m2_ev, 2 * (M2 * fb + s - 2))
                for gl, bank in ((0, A), (1, BB)):
                    if gl and s >= 1:
                        pe.wait_ge(l_s, STEPS * fb + s)
                    if not gl and 1 <= s < 3:
                        pe.wait_ge(g_s, STEPS * fb + s)
                    for c in range(CT):
                        last = mm(bank[:, :], W1[:, e % 2, c, FI * gl + P * it:FI * gl + P * (it + 1)],
                                  nfT[:, c, 512 * n:512 * (n + 1)], start=c == 0, stop=c == CT - 1)
                    last.then_inc(m1_mm, 1)

            def expert_down(fb, s):
                if s < 2:
                    return
                u, hh = divmod(s - 2, 2)
                e, n = divmod(u, NCH)
                if hh == 0:
                    pe.wait_ge(lo_s, STEPS * fb + 2 * u + 2)
                    pe.wait_ge(w2_s, NE * fb + e + 1)
                if s < STEPS:
                    pe.wait_ge(g_s, STEPS * fb + s + 1)
                else:
                    pe.wait_ge(m2_ev, 2 * (M2 * fb + s - 2))
                for q in range(2):
                    tok = P * (2 * hh + q)
                    k = 0
                    for it in range(CT):
                        for part in (act_hi, act_lo):
                            last = mm(A[:, E * q:E * (q + 1)], part[:, u % 2, it, tok:tok + P], W2[:, e % 2, it, :],
                                      start=k == 0, stop=k == 3)
                            k += 1
                last.then_inc(m2_mm, 1)

            def attention(b, fb):
                for j in range(HG):
                    scores(b, 0, j)
                for s in range(STEPS):
                    for j in range(HG):
                        if s + 1 < STEPS:
                            scores(b, s + 1, j)
                        if j == 0 and fb is not None:
                            expert_up(fb, s)
                        if j == 1:
                            values(b, s, 0)
                        if j == 2 and fb is not None:
                            expert_down(fb, s)
                        if j == 3:
                            values(b, s, 1)
                if fb is not None:
                    expert_down(fb, STEPS)
                    expert_down(fb, STEPS + 1)

            pe.wait_ge(c_ld, 16 * (CONST_LOADS))
            pe.wait_ge(c_set, N_CONST_SET)
            prep(0)
            exact(0)
            attention(0, None)
            with pe.Fori(1, B) as b:
                prep(b)
                exact(b)
                post(b - 1)
                attention(b, b - 1)
            post(B - 1)
            for s in range(STEPS + 2):
                if s < STEPS:
                    expert_up(B - 1, s)
                expert_down(B - 1, s)

        @block.scalar
        def _(act):
            def prep(b):
                act.wait_ge(xt_mm, 2 * b + 1)
                nc.scalar.copy(xnT[:, 0, :], S[:, 0, :]).then_inc(xnT_a, 1)

                def biased(i):
                    act.wait_ge(qk_mm, 4 * b + i + 1)
                    if i >= 2:
                        act.wait_ge(qk_sw, 4 * b + i - 1)
                        act.wait_ge(qk_cos, 4 * b + i - 1)
                    nc.scalar.activation(qb[i % 2], S[:, i % 2, :], ACT.Identity, bias=bqk_sb[:, i:i + 1]).then_inc(qk_b, 1)

                biased(0)
                for i in range(4):
                    if i < 3:
                        biased(i + 1)
                    act.wait_ge(qk_rot, 4 * b + i + 1)
                    if i >= 2:
                        act.wait_ge(scr_w[i % 2], 32 * b + 16)
                    nc.scalar.copy(parts[i % 2][:, 0, :], rot[i % 2]).then_inc(qk_p1, 1)
                    if i >= 1:
                        act.wait_ge(nrm_mm, 4 * b + i)
                    nc.scalar.activation(sq, rot[i % 2], ACT.Square).then_inc(qk_sq, 1)
                    act.wait_ge(qk_r1, 4 * b + i + 1)
                    nc.scalar.copy(parts[i % 2][:, 1, :], sw[i % 2]).then_inc(qk_p2, 1)

            def post(b):
                for t in range(TT):
                    act.wait_ge(xc_s, TT * b + t + 1)
                    if t:
                        act.wait_ge(ss_s, TT * b + t)
                    nc.scalar.activation(sqs[:, :], xc[:, t, :], ACT.Square, accum_out=ss[:, t:t + 1]).then_inc(ss_s, 1)
                act.wait_ge(nft_mm, 2 * b + 1)
                nc.scalar.copy(nfT[:, 0, :], A[:, :].bitcast(BF16)).then_inc(nfT_a, 1)
                act.wait_ge(dtop_s, b + 1)
                nc.scalar.activation(etop[:, :], dtop[:, :], ACT.Exp).then_inc(etop_s, 1)

            def exps(b, s, j):
                act.wait_ge(s_done, 128 * b + 4 * s + j + 1)
                if j == 0 and s >= 2:
                    act.wait_ge(av_done, STEPS * b + s - 1)
                nc.scalar.activation(probs[:, s % 2, j, :], S[:, j % 2, :], ACT.Exp, scale=SCALE).then_inc(exp_done, 1)

            def tanh(fb, s):
                act.wait_ge(g_s, STEPS * fb + s + 1)
                if s >= 2:
                    act.wait_ge(act_s, STEPS * fb + s - 1)
                nc.scalar.activation(th_sb[s % 2], g_sb[s % 2], ACT.Tanh, scale=ALPHA / 2).then_inc(th_s, 1)

            def attention(b, fb):
                for j in range(HG):
                    exps(b, 0, j)
                for s in range(STEPS):
                    if s + 1 < STEPS:
                        exps(b, s + 1, 0)
                        exps(b, s + 1, 1)
                    if fb is not None:
                        tanh(fb, s)
                    if s + 1 < STEPS:
                        exps(b, s + 1, 2)
                        exps(b, s + 1, 3)

            act.wait_ge(c_ld, 16 * (CONST_LOADS))
            prep(0)
            attention(0, None)
            with act.Fori(1, B) as b:
                prep(b)
                post(b - 1)
                attention(b, b - 1)
            post(B - 1)
            for s in range(STEPS):
                tanh(B - 1, s)

        @block.gpsimd
        def _(pool):
            def prep(b):
                pool.wait_ge(var1_s, b + 1)
                nc.gpsimd.tensor_tensor(rstd1[:, :], var1[:, :], half_pow[:, :], ALU.pow).then_inc(rstd1_s, 1)
                for i in range(4):
                    pool.wait_ge(qk_b, 4 * b + i + 1)
                    if i >= 2:
                        pool.wait_ge(qk_r1, 4 * b + i - 1)
                        pool.wait_ge(qk_sq, 4 * b + i - 1)
                    nc.gpsimd.tensor_tensor(rot[i % 2], qb[i % 2], cos_sb[:, :], ALU.mult).then_inc(qk_cos, 1)
                wait_apart(pool, (nsq_s, b + 1))
                nc.gpsimd.partition_all_reduce(nsqa[:, :], nsq2[:, :], P, bass.bass_isa.ReduceOp.max).then_inc(nsqa_s, 1)

            def normalise(b, g):
                G = NG * b + g
                pool.wait_ge(rec_r, 64 * (G + 1))
                nc.gpsimd.tensor_tensor(O[:, g, :], O[:, g, :], rec_b[:, :], ALU.mult).then_inc(on_s, 1)

            def post(b):
                pool.wait_ge(var2_s, b + 1)
                nc.gpsimd.tensor_tensor(rstd2[:, :], var2[:, :], half_pow[:, :], ALU.pow).then_inc(rstd2_s, 1)
                pool.wait_ge(ms_s, b + 1)
                nc.gpsimd.tensor_tensor(rrms[:, :], ms[:, :], half_pow[:, :], ALU.pow).then_inc(rrms_s, 1)

            def convert(fb, e):
                wait_apart(pool, (w2_ld[e % 2], 16 * (4 * fb + e // 2 + 1)), *[(m2_mm, M2 * fb + 4 * (e - 1))][:e // 2])
                nc.gpsimd.tensor_copy(W2[:, e % 2, :, :], W2b[:, e % 2, :, :]).then_inc(w2_s, 1)

            def low(fb, s):
                u, it = divmod(s, 2)
                if u >= 2:
                    pool.wait_ge(m2_mm, M2 * fb + 2 * (u - 1))
                pool.wait_ge(hi_s, STEPS * fb + s + 1)
                nc.gpsimd.tensor_tensor(act_lo[:, u % 2, it, :], act_sb[s % 2], act_hi[:, u % 2, it, :].bitcast(FP32),
                                        ALU.subtract).then_inc(lo_s, 1)

            def experts(b, fb):
                for s in range(STEPS):
                    if fb is not None:
                        if s == 0:
                            convert(fb, 0)
                            convert(fb, 1)
                        low(fb, s)
                        if s % 4 == 1 and s >= 5 and s // 4 + 1 < NE:
                            convert(fb, s // 4 + 1)
                    if b is not None and s >= KT and s % KT == 5:
                        normalise(b, s // KT - 1)
                if b is not None:
                    normalise(b, NG - 1)

            pool.wait_ge(c_ld, 16 * (CONST_LOADS))
            pool.wait_ge(c_set, N_CONST_SET)
            prep(0)
            experts(0, None)
            with pool.Fori(1, B) as b:
                prep(b)
                post(b - 1)
                experts(b, b - 1)
            post(B - 1)
            experts(None, B - 1)

        @block.vector
        def _(dve):
            v = nc.vector

            def norm_stats(src, st, mv, var, stat_s, aggr_s, var_s, b):
                for t in range(TT):
                    v.bn_stats(st[:, t, :], src[:, t, :]).then_inc(stat_s, 1)
                for t in range(TT):
                    wait_apart(dve, (stat_s, TT * b + t + 1))
                    v.bn_aggr(mv[:, t, :], st[:, t, :]).then_inc(aggr_s, 1)
                dve.wait_ge(aggr_s, TT * (b + 1))
                v.tensor_scalar(var[:, :], mv[:, :, 1], EPS, None, ALU.add).then_inc(var_s, 1)

            def prep(b):
                dve.wait_ge(x_ld, 16 * (b + 1))
                norm_stats(X, st1, mv1, var1, stat1, aggr1, var1_s, b)
                dve.wait_ge(rstd1_s, b + 1)
                if not isinstance(b, int):
                    dve.wait_ge(av_done, STEPS * b)
                for t in range(TT):
                    v.tensor_scalar(xn[:, t, :], X[:, t, :], mv1[:, t, 0:1], rstd1[:, t:t + 1],
                                    ALU.subtract, ALU.mult).then_inc(xn_s, 1)
                dve.wait_ge(xt_mm, 2 * b + 2)
                v.tensor_copy(xnT[:, 1, :], S[:, 1, :]).then_inc(xnT_v, 1)

                def r1(i):
                    dve.wait_ge(qk_p1, 4 * b + i + 1)
                    v.tensor_tensor(sw[i % 2], rot[i % 2], parts[i % 2][:, 0, :], ALU.subtract).then_inc(qk_r1, 1)

                def p3(i):
                    dve.wait_ge(qk_p2, 4 * b + i + 1)
                    v.tensor_tensor(parts[i % 2][:, 2, :], sw[i % 2], parts[i % 2][:, 1, :], ALU.subtract).then_inc(qk_p3, 1)

                def longest(i):
                    dve.wait_ge(nrm_mm, 4 * b + i + 1)
                    t, hf = divmod(i, 2)
                    v.reduce_max(nsq[:, t, 2 * hf:2 * hf + 1], A[:, :], AX_X).then_inc(nrm_red, 1)
                    v.reduce_max(nsq[:, t, 2 * hf + 1:2 * hf + 2], BB[:, :], AX_X).then_inc(nrm_red, 1)

                swap = [r ^ 1 for r in range(32)]
                for i in range(4):
                    wait_apart(dve, (qk_b, 4 * b + i + 1), *[(qk_p3, 4 * b + i - 1)][:i // 2])
                    v.stream_shuffle(sw[i % 2], qb[i % 2], swap).then_inc(qk_sw, 1)
                    dve.wait_ge(qk_sw, 4 * b + i + 1)
                    v.tensor_tensor(sw[i % 2], sw[i % 2], sin_sb[:, :], ALU.mult).then_inc(qk_sin, 1)
                    if i >= 1:
                        r1(i - 1)
                    dve.wait_ge(qk_cos, 4 * b + i + 1)
                    dve.wait_ge(qk_sin, 4 * b + i + 1)
                    v.tensor_tensor(rot[i % 2], rot[i % 2], sw[i % 2], ALU.add).then_inc(qk_rot, 1)
                    if i >= 1:
                        p3(i - 1)
                        longest(i - 1)
                r1(3)
                p3(3)
                longest(3)
                dve.wait_ge(nrm_red, 8 * (b + 1))
                v.reduce_max(nsq2[:, :], nsq[:, :, :], AX_X).then_inc(nsq_s, 1)
                for hf in range(2):
                    dve.wait_ge(v_mm, 2 * b + hf + 1)
                    v.tensor_tensor(V[:, 4 * hf:4 * hf + 4, :, 0:HD],
                                    S[:, hf, :].rearrange("p (t h d) -> p t h d", t=4, h=H),
                                    bv_sb[:, :].rearrange("p (h d) -> p h d", h=H)[:, None, :, :].to_broadcast([P, 4, H, HD]),
                                    ALU.add).then_inc(v_done, 1)
                dve.wait_ge(nsqa_s, b + 1)
                v.tensor_tensor(bound[:, :], nsqa[:, 0:1], nsqa[:, 1:2], ALU.mult).then_inc(bound_s, 1)
                dve.wait_ge(bound_s, b + 1)
                v.tensor_scalar(exact_flag[:, bass.ds(b, 1)], bound[:, :], (safe_score / SCALE) ** 2 / 1.05 if safe_score > 0 else -1.0,
                                None, ALU.is_gt).then_inc(flag_s, 1)

            def exact(b):
                wait_apart(dve, (flag_s, b + 1), *([] if isinstance(b, int) else [(m_w, 16 * b)]))
                flag = dve.value_load(exact_flag[0:1, bass.ds(b, 1)], min_val=0, max_val=1)
                with dve.If(flag > 0):
                    for i in range(128):
                        dve.wait_ge(ex_mm, 128 * b + i + 1)
                        v.reduce_max(mx[:, i % 8, i // 8:i // 8 + 1], S[:, i % 2, :], AX_X).then_inc(ex_red, 1)
                    dve.wait_ge(ex_t, b + 1)
                    v.tensor_scalar(Mt[:, 0, :], S[0:H, 0, :], -1.0, None, ALU.mult).then_inc(m_set, 1)
                    dve.wait_ge(m_set, 2 * b + 1)
                    v.scalar_tensor_tensor(Mt[:, 1, :], S[0:H, 0, :], -1.0, Mt[:, 0, :], ALU.mult, ALU.subtract).then_inc(m_set, 1)
                with dve.If(flag < 1):
                    v.memset(Mt[:, :, :], 0.0).then_inc(m_set, 1)
                    dve.sem_inc(m_set, 1)
                    dve.sem_inc(ex_red, 128)

            def post(b):
                dve.wait_ge(x1_ld, 16 * (b + 1))
                for hf in range(2):
                    dve.wait_ge(y_mm, 2 * b + hf + 1)
                    xh = X1[:, 4 * hf:4 * hf + 4, :].rearrange("p t c -> p (t c)")
                    v.tensor_tensor(xh, S[:, hf, :], xh, ALU.add).then_inc(x1_s, 1)
                dve.wait_ge(x1_s, 2 * (b + 1))
                norm_stats(X1, st2, mv2, var2, stat2, aggr2, var2_s, b)
                dve.wait_ge(rstd2_s, b + 1)
                for t in range(TT):
                    v.tensor_scalar(xc[:, t, :], X1[:, t, :], mv2[:, t, 0:1], rstd2[:, t:t + 1],
                                    ALU.subtract, ALU.mult).then_inc(xc_s, 1)
                dve.wait_ge(ss_s, TT * (b + 1))
                v.tensor_scalar(ms[:, :], ss[:, :], 1.0 / E, EPS, ALU.mult, ALU.add).then_inc(ms_s, 1)
                if not isinstance(b, int):
                    for k in range(2):
                        dve.wait_ge(scr_w[k], 32 * (b + 2))
                dve.wait_ge(rrms_s, b + 1)
                for t in range(TT):
                    v.scalar_tensor_tensor(nf[:, t, :], xc[:, t, :], rrms[:, t:t + 1], nw_sb[:, :],
                                           ALU.mult, ALU.mult).then_inc(nf_s, 1)
                dve.wait_ge(nft_mm, 2 * b + 2)
                v.tensor_copy(nfT[:, 1, :], BB[:, :].bitcast(BF16)).then_inc(nfT_v, 1)

                steps = [0]

                def link(ins):
                    steps[0] += 1
                    ins.then_inc(gating, 1)
                    dve.wait_ge(gating, GATING * b + steps[0])

                def over_experts(a):
                    return a[:, :, None].to_broadcast([P, TT, NE])

                def first_of(onehot, logits, top):
                    link(v.reduce_max(top[:, :], logits, AX_X))
                    link(v.tensor_tensor(pick[:, :, :], logits, over_experts(top), ALU.is_equal))
                    link(v.tensor_tensor(pick[:, :, :], pick[:, :, :], rank[:, None, :].to_broadcast([P, TT, NE]), ALU.mult))
                    link(v.reduce_max(pickm[:, :], pick[:, :, :], AX_X))
                    link(v.tensor_tensor(onehot[:, :, :], pick[:, :, :], over_experts(pickm), ALU.is_equal))

                GATING = 18
                dve.wait_ge(lg_mm, b + 1)
                link(v.tensor_tensor(lgb[:, :, :], OP[:, 0:TT * NE].rearrange("p (t e) -> p t e", e=NE),
                                     gate_b_sb[:, None, :].to_broadcast([P, TT, NE]), ALU.add))
                link(v.tensor_copy(lgt[:, :, :], lgb[:, :, :]))
                first_of(oh1, lgt[:, :, :], top1)
                link(v.scalar_tensor_tensor(lg2[:, :, :], oh1[:, :, :], -3.0e38, lgt[:, :, :], ALU.mult, ALU.add))
                first_of(oh2, lg2[:, :, :], top2)
                v.tensor_tensor(dtop[:, :], top2[:, :], top1[:, :], ALU.subtract).then_inc(dtop_s, 1)
                dve.wait_ge(etop_s, b + 1)
                link(v.tensor_scalar(w_2[:, :], etop[:, :], 1.0, None, ALU.add))
                link(v.reciprocal(w_1[:, :], w_2[:, :]))
                link(v.tensor_tensor(w_2[:, :], w_1[:, :], etop[:, :], ALU.mult))
                link(v.tensor_tensor(oh1[:, :, :], oh1[:, :, :], over_experts(w_1), ALU.mult))
                link(v.tensor_tensor(oh2[:, :, :], oh2[:, :, :], over_experts(w_2), ALU.mult))
                assert steps[0] == GATING
                v.tensor_tensor(comb[:, :, :], oh1[:, :, :], oh2[:, :, :], ALU.add).then_inc(comb_s, 1)
                dve.wait_ge(comb_s, 3 * b + 1)
                v.tensor_scalar(combh[:, :, :], comb[:, :, :], 0.5, None, ALU.mult).then_inc(comb_s, 2)
                dve.wait_ge(ct_mm, b + 1)
                v.tensor_copy(combT, OP[0:NE, :]).then_inc(combT_s, 1)
                for hf in range(2):
                    dve.wait_ge(b2_mm, 2 * b + hf + 1)
                    v.tensor_copy(acc[:, 4 * hf:4 * hf + 4, :].rearrange("p t c -> p (t c)"), S[:, hf, :]).then_inc(acc_s, 1)

            def output_out(b, g):
                G = NG * b + g
                dve.wait_ge(av_done, STEPS * b + KT * (g + 1))
                v.tensor_copy(O[:, g, :], OP[:, :]).then_inc(o_ev, 1)

            def reciprocals(b, g):
                G = NG * b + g
                dve.wait_ge(sum_r, 16 * (G + 1))
                v.reciprocal(rec_c[:, :], sums_c[:, :]).then_inc(rec_s, 1)

            def up_out(fb, s):
                u, it = divmod(s, 2)
                e = u // NCH
                n = STEPS * fb + s
                dve.wait_ge(m1_mm, 2 * n + 1)
                if s >= 2:
                    dve.wait_ge(act_s, n - 1)
                v.tensor_scalar(g_sb[s % 2], A[:, :], b1f[:, e, 0, it:it + 1], LIMIT, ALU.add, ALU.min).then_inc(g_s, 1)
                dve.wait_ge(m1_mm, 2 * n + 2)
                v.tensor_scalar(l_sb[s % 2], BB[:, :], b1f[:, e, 1, it:it + 1], 1.0 - LIMIT, ALU.add, ALU.max).then_inc(l_s, 1)

            def down_out(fb, s):
                if s < 2:
                    return
                u, hh = divmod(s - 2, 2)
                e, n = divmod(u, NCH)
                m = M2 * fb + s - 2
                dve.wait_ge(m2_mm, m + 1)
                if s == 2:
                    dve.wait_ge(acc_s, 2 * (fb + 1))
                else:
                    dve.wait_ge(m2_ev, 2 * m)
                for q in range(2):
                    t = 4 * n + 2 * hh + q
                    v.scalar_tensor_tensor(acc[:, t, :], A[:, E * q:E * (q + 1)], combh[:, t, e:e + 1], acc[:, t, :],
                                           ALU.mult, ALU.add).then_inc(m2_ev, 1)

            def activation(fb, s):
                u, it = divmod(s, 2)
                n = STEPS * fb + s
                dve.wait_ge(th_s, n + 1)
                v.scalar_tensor_tensor(th_sb[s % 2], th_sb[s % 2], 1.0, g_sb[s % 2], ALU.add, ALU.mult).then_inc(t1_s, 1)
                dve.wait_ge(t1_s, n + 1)
                dve.wait_ge(l_s, n + 1)
                if s >= 2:
                    dve.wait_ge(lo_s, n - 1)
                v.scalar_tensor_tensor(act_sb[s % 2], l_sb[s % 2], 1.0 + LIMIT, th_sb[s % 2], ALU.min, ALU.mult).then_inc(act_s, 1)
                dve.wait_ge(act_s, n + 1)
                if u >= 2:
                    dve.wait_ge(m2_mm, M2 * fb + 2 * (u - 1))
                v.tensor_copy(act_hi[:, u % 2, it, :], act_sb[s % 2]).then_inc(hi_s, 1)

            def attention(b, fb):
                for s in range(STEPS):
                    g, kt = divmod(s, KT)
                    if kt == 0 and g:
                        output_out(b, g - 1)
                    if fb is not None:
                        up_out(fb, s)
                        down_out(fb, s)
                        activation(fb, s)
                    if kt == 3 and g:
                        reciprocals(b, g - 1)
                output_out(b, NG - 1)
                if fb is not None:
                    down_out(fb, STEPS)
                    down_out(fb, STEPS + 1)
                    final(fb)
                reciprocals(b, NG - 1)

            def final(fb):
                accv = acc[:, :, :].rearrange("p t c -> p (t c)")
                cb = nfT[:, :, :].rearrange("p t c -> p (t c)")
                xcv = xc[:, :, :].rearrange("p t c -> p (t c)")
                x1v = X1[:, :, :].rearrange("p t c -> p (t c)")
                dve.wait_ge(m2_ev, 2 * M2 * (fb + 1))
                v.tensor_copy(cb, accv).then_inc(cb_s, 1)
                dve.wait_ge(cb_s, fb + 1)
                v.tensor_tensor(cb, cb, xcv, ALU.add).then_inc(fo_s, 1)
                dve.wait_ge(fo_s, fb + 1)
                for hf in range(2):
                    r = slice(L * hf, L * (hf + 1))
                    v.tensor_tensor(accv[:, r], x1v[:, r], cb[:, r], ALU.add).then_inc(x2_s, 1)

            v.memset(half_pow[:, :], -0.5).then_inc(c_set, 1)
            v.memset(V[:, :, :, HD:VW], 1.0).then_inc(c_set, 1)
            v.memset(Ks[SROWS:SROWS + MROWS, :, :, :], 1.0).then_inc(c_set, 1)
            v.memset(OP[:, :], 0.0).then_inc(c_set, 1)
            dve.wait_ge(c_ld, 16 * (CONST_LOADS))
            v.tensor_copy(identb[:, :], ident[:, :]).then_inc(c_set, 1)
            v.tensor_copy(same_head[:, :], th_sb[0][:, 0:P]).then_inc(c_set, 1)
            v.tensor_copy(b1f[:, :, 0, :], b1_sb[:, :, 0, :]).then_inc(c_set, 1)
            v.tensor_scalar(b1f[:, :, 1, :], b1_sb[:, :, 1, :], 1.0, None, ALU.add).then_inc(c_set, 1)
            v.tensor_copy(b2f[:, :], b2_sb[:, :]).then_inc(c_set, 1)
            dve.wait_ge(c_set, N_CONST_SET)
            prep(0)
            exact(0)
            attention(0, None)
            with dve.Fori(1, B) as b:
                prep(b)
                exact(b)
                post(b - 1)
                attention(b, b - 1)
            post(B - 1)
            for s in range(STEPS):
                up_out(B - 1, s)
                down_out(B - 1, s)
                activation(B - 1, s)
            down_out(B - 1, STEPS)
            down_out(B - 1, STEPS + 1)
            final(B - 1)


def layouts(np, d):
    f = lambda n: np.asarray(d[n])
    wq, wk, wv, wo = (f(f"L0_attn_W{n}") for n in "qkvo")
    wo_p = np.zeros((NG, HG, 32, E), wo.dtype)
    wo_p[:, :, :HD, :] = wo.T.reshape(NG, HG, HD, E)
    wo_p[0, 0, HD, :] = f("L0_attn_bo")
    w1 = f("L0_ffn_mlp1_weight").reshape(NE, CT, P, 2, CT, P)
    w2 = f("L0_ffn_mlp2_weight").reshape(NE, E, CT, P)
    b1 = f("L0_ffn_mlp1_bias").reshape(NE, CT, P, 2)
    return {
        "x": f("L0_attn_x"),
        "wqk": np.concatenate([wq.T, wk.T], axis=1),
        "bqk": np.concatenate([f("L0_attn_bq"), f("L0_attn_bk")]).reshape(4, P).T,
        "wv": wv.T,
        "bv": f("L0_attn_bv"),
        "wo": wo_p.reshape(NG, P, E),
        "nw": f("L0_ffn_norm_weight"),
        "gate": f("L0_ffn_gate_weight").T,
        "gate_b": f("L0_ffn_gate_bias"),
        "w1": w1.transpose(0, 5, 4, 3, 1, 2).reshape(NE, P, CT, 2 * FI),
        "b1": b1.transpose(2, 0, 3, 1),
        "w2": w2.transpose(0, 3, 2, 1),
        "b2": f("L0_ffn_mlp2_bias"),
    }


def constants(np):
    inv = (1.0 / np.float32(10000.0) ** (np.arange(0, HD, 2, dtype=np.float32) / np.float32(HD))).astype(np.float32)
    ang = (np.arange(L, dtype=np.float32)[:, None] * inv[None, :]).astype(np.float32)
    ang = np.tile(np.repeat(ang, 2, axis=1).T, (P // HD, 1))
    sign = np.where(np.arange(P) % 2 == 0, -1.0, 1.0).astype(np.float32)[:, None]
    head = np.arange(P) // HD
    return {
        "rope": np.stack([np.cos(ang), np.sin(ang) * sign]).astype(np.float32),
        "ident_in": np.eye(P, dtype=np.float32),
        "heads_in": (head[:, None] == head[None, :]).astype(np.float32),
        "rank_in": np.arange(NE, 0, -1).astype(np.float32),
    }


def kernel(**inputs):
    import numpy as _np
    import concourse.bacc as _bacc
    from concourse.bass_utils import run_bass_kernel_spmd as _run

    nc = _bacc.Bacc("TRN2", target_bir_lowering=False, num_devices=1)
    arrays, args = {}, {}
    for name, a in {**layouts(_np, inputs), **constants(_np)}.items():
        a = _np.ascontiguousarray(a)
        arrays[f"in_{name}"] = a
        args[name] = nc.dram_tensor(f"in_{name}", a.shape, mybir.dt.from_np(a.dtype), kind="ExternalInput").ap()
    args["out"] = nc.dram_tensor("out_0", (B, L, E), FP32, kind="ExternalOutput").ap()
    block_kernel(nc, **args)
    r = _run(nc, [arrays], core_ids=[0])
    return r.results[0]["out_0"]
```

```python
from contextlib import ExitStack

import concourse.bass as bass
from concourse import mybir

FP32 = mybir.dt.float32
FP32R = mybir.dt.float32r
BF16 = mybir.dt.bfloat16
INT32 = mybir.dt.int32
ALU = mybir.AluOpType
ACT = mybir.ActivationFunctionType
AX_X = mybir.AxisListType.X

P = 128
B, L, E = 4, 1024, 256
H, HD = 16, 16
NE, TOPK, FI = 8, 2, 256
LIMIT, ALPHA, EPS = 7.0, 1.702, 1e-5
CT = E // P
TT = L // P
HG = 4
NG = H // HG
KT = L // P
STEPS = NG * KT
C = 512
NCH = L // C
TC = C // P
NF = 2 * NE
SROWS = 6 * HD
MROWS = 2
VW = HD + 1
SCALE = HD ** -0.5
SAFE_SCORE = 60.0
Q_PARTS = (0, 0, 0, 1, 1, 2)
K_PARTS = (0, 1, 2, 0, 1, 0)


def looped(value):
    return not isinstance(value, int)


def block_kernel(nc, x, wqk, bqk, wv, bv, wo, bo, nw, gate, gate_b, w1, b1, w2, b2, rope, ident_in, heads_in, rank_in,
                 out, safe_score=SAFE_SCORE):

    PREP = {}
    POST = {}
    EXPERTS = {}

    def place(table, step, half, *stages):
        table.setdefault((step, half), []).extend(stages)

    place(PREP, 0, 0, ("x_in", 0))
    place(PREP, 1, 0, ("stats1", 0))
    place(PREP, 1, 1, ("rstd1", 0))
    place(PREP, 2, 1, ("xn", 0))
    place(PREP, 3, 1, ("xT", 0))
    place(PREP, 4, 0, ("xT", 1))
    for a, t in enumerate((5, 8, 11, 15)):
        place(PREP, t, 0, ("qk", a))
        place(PREP, t, 1, ("rope", a))
        place(PREP, t + 2, 0, ("part1", a))
        place(PREP, t + 2, 1, ("length", a))
        place(PREP, t + 3, 0, ("part2", a))
        place(PREP, t + 3, 1, ("part3", a))
    place(PREP, 18, 0, ("v", 0))
    place(PREP, 21, 0, ("v", 1))
    place(PREP, 19, 1, ("guard", 0))

    place(POST, 0, 1, ("x1_in", 0))
    place(POST, 2, 0, ("x1_b", 0))
    place(POST, 6, 0, ("wo", 0))
    place(POST, 7, 0, ("wo", 1))
    place(POST, 8, 0, ("stats2", 0))
    place(POST, 8, 1, ("rstd2", 0))
    place(POST, 9, 1, ("xc", 0))
    place(POST, 10, 0, ("ss", 0))
    place(POST, 10, 1, ("ms", 0))
    place(POST, 11, 0, ("rrms", 0))
    place(POST, 11, 1, ("nf", 0))
    place(POST, 12, 0, ("nfT", 0))
    place(POST, 12, 1, ("logits", 0))
    place(POST, 13, 0, ("gates1", 0))
    place(POST, 13, 1, ("etop", 0))
    place(POST, 14, 0, ("gates2", 0))
    place(POST, 16, 0, ("combT", 0))
    place(POST, 16, 1, ("b2", 0))
    place(POST, 17, 0, ("b2", 1))

    FFN0, LAG = 13, 4
    for f in range(NF + LAG):
        step = FFN0 + f * 3 // 2
        if f >= LAG:
            place(EXPERTS, step, 0, ("down", f - LAG))
        if 1 <= f <= NF:
            place(EXPERTS, step, 0, ("tanh", f - 1))
            place(EXPERTS, step, 1, ("hidden", f - 1))
        if f < NF:
            place(EXPERTS, step, 1, ("up", f))
    FINAL = step
    place(EXPERTS, FINAL, 1, ("final", 0))
    FILLS = ("xT", "qk", "v", "length", "wo", "nfT", "logits", "combT", "b2")
    PREP_FILLS = sum(st in FILLS for l in PREP.values() for st, _ in l)
    POST_FILLS = sum(st in FILLS for l in POST.values() for st, _ in l)

    class Beside:

        def at(self, base, b, n, prep, post):
            self.n, self.last = base, None
            if looped(base) or base:
                for step in range(STEPS):
                    for half in range(2):
                        for _ in self.stages(b, n, step, half, prep, post, False):
                            pass
                self.n = base

        def stages(self, b, n, step, place, prep, post, late):
            todo = []
            after, before, before2 = (b + 1, n), ((b, n - 1) if n else (b - 1, NCH - 1)), (b - 1, n)
            if late:
                todo += [(st, a, before2) for st, a in EXPERTS.get((step + STEPS, place), [])]
            if prep:
                todo += [(st, a, after) for st, a in PREP.get((step, place), [])]
            if post:
                todo += [(st, a, before) for st, a in POST.get((step, place), [])]
                todo += [(st, a, before) for st, a in EXPERTS.get((step, place), [])]
            for st, a, (batch, chunk) in todo:
                k = (self.n, self.last)
                if st in FILLS:
                    self.n, self.last = self.n + 1, (st, a, NCH * batch + chunk)
                yield st, a, batch, chunk, k

    ctx = ExitStack()
    with ctx:
        def sb(name, shape, dt):
            return ctx.enter_context(nc.sbuf_tensor(name, shape, dt))

        def ps(name, shape, dt):
            return ctx.enter_context(nc.psum_tensor(name, shape, dt))

        def sem(name):
            return ctx.enter_context(nc.semaphore(name))

        def scratch(name, shape, dt):
            return nc.dram_tensor(name, shape, dt, kind="Internal").ap()

        qk_scr = scratch("qk_scr", (B, 2, 3, E, L), BF16)
        m_scr = scratch("m_scr", (B, MROWS, H, L), BF16)
        o_scr = scratch("o_scr", (B * NCH, NG, P, C), FP32)
        rec_scr = scratch("rec_scr", (B * NCH, NG, HG, C), FP32)

        wqk_sb = sb("wqk_sb", [P, CT, 2 * E], FP32)
        bqk_sb = sb("bqk_sb", [P, 4], FP32)
        wv_sb = sb("wv_sb", [P, CT, E], FP32)
        bv_sb = sb("bv_sb", [P, E], FP32)
        wo_sb = sb("wo_sb", [P, CT, E], FP32)
        bo_sb = sb("bo_sb", [P, E], FP32)
        nw_sb = sb("nw_sb", [P, E], FP32)
        gate_sb = sb("gate_sb", [P, CT, NE], BF16)
        gate_b_sb = sb("gate_b_sb", [P, NE], BF16)
        b1_sb = sb("b1_sb", [P, NE, 2, CT], BF16)
        b1f = sb("b1f", [P, NE, 2, CT], FP32)
        b2_sb = sb("b2_sb", [NE, E], BF16)
        b2f = sb("b2f", [NE, E], FP32)
        cos_sb = sb("cos_sb", [P, L], FP32)
        sin_sb = sb("sin_sb", [P, L], FP32)
        ident = sb("ident", [P, P], FP32)
        identb = sb("identb", [P, P], BF16)
        same_head_f = sb("same_head_f", [P, P], FP32)
        same_head = sb("same_head", [P, P], BF16)
        rank = sb("rank", [P, NE], FP32)
        half_pow = sb("half_pow", [P, TC], FP32)

        X = sb("X", [P, TC, E], FP32)
        xn = sb("xn", [P, TC, E], FP32)
        xnT = sb("xnT", [P, CT, C], FP32)
        qb = sb("qb", [P, 2, C], FP32)
        sw = sb("sw", [P, 2, C], FP32)
        rot = sb("rot", [P, 2, C], FP32)
        parts = sb("parts", [P, 2, 3, C], BF16)
        sq = sb("sq", [P, C], BF16)
        Vn = sb("Vn", [P, KT, H, HD], FP32)

        V = sb("V", [P, KT, H, VW], FP32)
        Qs = sb("Qs", [P, 2, HG, C], BF16)
        Ks = sb("Ks", [P, 2, HG, L], BF16)
        probs = sb("probs", [P, 2, HG * C], FP32)
        O = sb("O", [P, 2, C], FP32)
        Op = sb("Op", [P, CT, C], FP32)
        rec_b = sb("rec_b", [P, C], FP32)
        sums_c = sb("sums_c", [P, 16], FP32)
        rec_c = sb("rec_c", [P, 16], FP32)
        Mt = sb("Mt", [H, MROWS, L], BF16)
        mx = sb("mx", [P, TT, H], FP32)

        X1s = sb("X1s", [P, 2, TC, E], FP32)
        xc = sb("xc", [P, 2, TC, E], BF16)
        nf = sb("nf", [P, TC, E], BF16)
        x2b = sb("x2b", [P, TC, E], BF16)
        nfT = sb("nfT", [P, CT, C], BF16)
        acc = sb("acc", [P, TC, E], FP32)
        combT = sb("combT", [NE, C], FP32)
        W1 = sb("W1", [P, 2, CT, 2 * FI], BF16)
        W2b = sb("W2b", [P, 2, CT * E], BF16)
        W2 = sb("W2", [P, 2, CT * E], FP32R)
        act_hi = sb("act_hi", [P, 2, CT, C], FP32R)
        act_lo = sb("act_lo", [P, 2, CT, C], FP32R)
        g_sb = sb("g_sb", [P, 2, C], FP32)
        l_sb = sb("l_sb", [P, 2, C], FP32)
        th_sb = sb("th_sb", [P, 2, C], FP32)
        act_sb = sb("act_sb", [P, 2, C], FP32)

        st1, st2 = sb("st1", [P, TC, 6], FP32), sb("st2", [P, TC, 6], FP32)
        mv1, mv2 = sb("mv1", [P, TC, 2], FP32), sb("mv2", [P, TC, 2], FP32)
        var1, rstd1, var2, rstd2, ss, ms, rrms, top1, top2, pickm, dtop, etop, w_1, w_2 = (
            sb(n, [P, TC], FP32) for n in ("var1", "rstd1", "var2", "rstd2", "ss", "ms", "rrms", "top1", "top2",
                                           "pickm", "dtop", "etop", "w_1", "w_2"))
        sqs = sb("sqs", [P, E], FP32)
        nsq = sb("nsq", [P, 2, 4], FP32)
        nsq2 = sb("nsq2", [P, 2], FP32)
        nsqa = sb("nsqa", [P, 2], FP32)
        bound = sb("bound", [P, 1], FP32)
        exact_flag = sb("exact_flag", [P, B], INT32)
        lgb = sb("lgb", [P, TC, NE], BF16)
        lgt, pick, oh1, oh2, lg2, comb, combh = (
            sb(n, [P, TC, NE], FP32) for n in ("lgt", "pick", "oh1", "oh2", "lg2", "comb", "combh"))

        S = ps("S", [P, 2, 2 * C], FP32)
        OP = ps("OP", [P, C], FP32)
        A = ps("A", [P, C], FP32)
        BB = ps("BB", [P, C], FP32)
        D = ps("D", [P, C], FP32)

        c_ld, c_set, passed = sem("c_ld"), sem("c_set"), sem("passed")
        d_full = sem("d_full")
        x_ld, stat1, aggr1, var1_s, rstd1_s, xn_s, xnT_s = (
            sem(n) for n in ("x_ld", "stat1", "aggr1", "var1_s", "rstd1_s", "xn_s", "xnT_s"))
        qk_b, qk_sw, qk_cos, qk_sin, qk_rot, qk_p1, qk_sq, qk_r1, qk_p2, qk_p3 = (
            sem(n) for n in ("qk_b", "qk_sw", "qk_cos", "qk_sin", "qk_rot", "qk_p1", "qk_sq", "qk_r1", "qk_p2", "qk_p3"))
        scr_w = [sem("scr_w0"), sem("scr_w1")]
        nrm_red, nsq_s, nsqa_s, bound_s, flag_s = (sem(n) for n in ("nrm_red", "nsq_s", "nsqa_s", "bound_s", "flag_s"))
        vn_s, v_s = sem("vn_s"), sem("v_s")
        ex_ld = [sem("ex_ld0"), sem("ex_ld1")]
        ex_mm, ex_red, ex_t, m_set, m_w, m_zero = (sem(n) for n in ("ex_mm", "ex_red", "ex_t", "m_set", "m_w", "m_zero"))
        st_ld = [sem("st_ld0"), sem("st_ld1")]
        s_done, exp_done, av_done = sem("s_done"), sem("exp_done"), sem("av_done")
        o_ev, o_w, o_r, sum_r, rec_s, rec_w, rec_r, on_s = (
            sem(n) for n in ("o_ev", "o_w", "o_r", "sum_r", "rec_s", "rec_w", "rec_r", "on_s"))
        x1_ld, x1_b, x1_s, stat2, aggr2, var2_s, rstd2_s, xc_s, ss_s, ms_s, rrms_s, nf_s, nfT_s = (
            sem(n) for n in ("x1_ld", "x1_b", "x1_s", "stat2", "aggr2", "var2_s", "rstd2_s", "xc_s", "ss_s", "ms_s",
                             "rrms_s", "nf_s", "nfT_s"))
        gating, dtop_s, etop_s, comb_s, combT_s, acc_s = (
            sem(n) for n in ("gating", "dtop_s", "etop_s", "comb_s", "combT_s", "acc_s"))
        w1_ld, w2_ld = [sem("w1_ld0"), sem("w1_ld1")], [sem("w2_ld0"), sem("w2_ld1")]
        w2_s, m1_mm, g_s, l_s, th_s, t1_s, act_s, hi_s, lo_s, m2_mm, m2_ev = (
            sem(n) for n in ("w2_s", "m1_mm", "g_s", "l_s", "th_s", "t1_s", "act_s", "hi_s", "lo_s", "m2_mm", "m2_ev"))
        cb_s, fo_s, x2_s, out_w = sem("cb_s"), sem("fo_s"), sem("x2_s"), sem("out_w")

        N_LOADS = 16
        N_CONST_SET = 10
        STACK = 16 * (2 * len(Q_PARTS) + 1)
        EX_STACK = 16 * 2 * len(Q_PARTS)
        GATES1, GATING = 13, 18
        PAIRS = 2 * STEPS

        x_v = x.rearrange("b (n t p) c -> (b n) p t c", p=P, t=TC)
        out_v = out.rearrange("b (n t p) c -> (b n) p t c", p=P, t=TC)

        def wait_apart(engine, *waits):
            for signal, value in waits:
                engine.wait_ge(signal, value)
                engine.sem_inc(passed, 1)

        FILLED0 = NCH * PREP_FILLS
        FILLED1 = FILLED0 + NCH * PREP_FILLS + POST_FILLS
        LOOP_FILLS = NCH * (PREP_FILLS + POST_FILLS)
        FILLED3 = FILLED1 + 2 * LOOP_FILLS
        FILLED4 = FILLED3 + NCH * POST_FILLS

        def run(engine, beside, stage, attend, start, turn):
            beside.at(0, 0, 0, False, False)
            for n in range(NCH):
                for step in range(STEPS):
                    for place in range(2):
                        for now in beside.stages(-1, n, step, place, True, False, False):
                            stage(*now)
            start()
            turn(0)

            def body(b, prep, base):
                beside.at(base, b - 1, NCH - 1, True, looped(b) or b >= 1)
                for n in range(NCH):
                    w = NCH * b + n
                    for s in range(STEPS):
                        def aside(place):
                            for now in beside.stages(b, n, s, place, prep, looped(b) or w >= 1, looped(b) or w >= 2):
                                stage(*now)
                        attend(b, n, s, prep, aside)
                if prep:
                    turn(b + 1)

            body(0, True, FILLED0)
            with engine.Fori(1, B - 1) as b:
                body(b, True, FILLED1 + LOOP_FILLS * (b - 1))
            body(B - 1, False, FILLED3)
            beside.at(FILLED4, B - 1, NCH - 1, False, True)
            for step in range(FINAL + 1):
                for place in range(2):
                    attend(B, 0, step, False, None, place)
                    left = (B, 0, step, place, False, True, True) if step < STEPS else (B, 1, step - STEPS, place, False, False, True)
                    for now in beside.stages(*left):
                        stage(*now)

        block = ctx.enter_context(nc.Block())

        @block.sync
        def _(sp):
            loads = (
                (wqk_sb[:, :, :], wqk.rearrange("(c p) n -> p c n", p=P)), (bqk_sb[:, :], bqk),
                (wv_sb[:, :, :], wv.rearrange("(c p) n -> p c n", p=P)), (bv_sb[:, :], bv[None, :].to_broadcast([P, E])),
                (wo_sb[:, :, :], wo.rearrange("(c p) n -> p c n", p=P)), (bo_sb[:, :], bo[None, :].to_broadcast([P, E])),
                (nw_sb[:, :], nw[None, :].to_broadcast([P, E])),
                (gate_sb[:, :, :], gate.rearrange("(c p) n -> p c n", p=P)),
                (gate_b_sb[:, :], gate_b[None, :].to_broadcast([P, NE])),
                (b1_sb[:, :, :, :], b1), (b2_sb[:, :], b2), (cos_sb[:, :], rope[0]), (sin_sb[:, :], rope[1]),
                (ident[:, :], ident_in), (rank[:, :], rank_in[None, :].to_broadcast([P, NE])), (same_head_f[:, :], heads_in),
            )
            assert len(loads) == N_LOADS

            def stack(b, n, g, signal, shifts):
                for blk, (qp, kp) in enumerate(zip(Q_PARTS, K_PARTS)):
                    rows, ch = slice(HD * blk, HD * (blk + 1)), slice(HG * HD * g, HG * HD * (g + 1))
                    sp.dma_start(Qs[rows, g % 2, :, :],
                                 qk_scr[b, 0, qp, ch, C * n:C * (n + 1)].rearrange("(j d) t -> d j t", d=HD)).then_inc(signal, 16)
                    sp.dma_start(Ks[rows, g % 2, :, :],
                                 qk_scr[b, 1, kp, ch, :].rearrange("(j d) t -> d j t", d=HD)).then_inc(signal, 16)
                if shifts:
                    sp.dma_start(Qs[SROWS:SROWS + MROWS, g % 2, :, :],
                                 m_scr[b, :, HG * g:HG * (g + 1), C * n:C * (n + 1)]).then_inc(signal, 16)

            def flag_of(b):
                return sp.value_load(exact_flag[0:1, bass.ds(b, 1)], min_val=0, max_val=1)

            def stage(st, a, bb, n, filling):
                k = filling[0]
                u = NCH * bb + n
                if st == "x_in":
                    if looped(u) or u >= 1:
                        sp.wait_ge(xn_s, TC * u)
                    sp.dma_start(X[:, :, :], x_v[bass.ds(u, 1)].rearrange("o p t c -> (o p) t c")).then_inc(x_ld, 16)
                elif st == "part3":
                    sp.wait_ge(qk_p3, 4 * u + a + 1)
                    sp.dma_start(qk_scr[bb, a // 2, :, P * (a % 2):P * (a % 2 + 1), C * n:C * (n + 1)]
                                 .rearrange("a p t -> p a t"), parts[:, a % 2, :, :]).then_inc(scr_w[a % 2], 16)
                elif st == "x1_in":
                    if looped(bb) or bb:
                        sp.wait_ge(x2_s, 2 * (u - 1))
                    sp.dma_start(X1s[:, n, :, :], x_v[bass.ds(u, 1)].rearrange("o p t c -> (o p) t c")).then_inc(x1_ld, 16)
                elif st == "up":
                    e, it = divmod(a, 2)
                    if it == 1 and e + 2 < NE:
                        wait_apart(sp, (m1_mm, 4 * NE * u + 4 * (e + 1)), (w2_s, NE * u + e + 1))
                        load_expert(e + 2)
                    if a == NF - 1:
                        wait_apart(sp, (m1_mm, 4 * NE * (u + 1)), (w2_s, NE * (u + 1)))
                        load_expert(0)
                        load_expert(1)
                elif st == "final":
                    sp.wait_ge(x2_s, 2 * (u + 1))
                    sp.dma_start(out_v[bass.ds(u, 1)].rearrange("o p t c -> (o p) t c"), acc[:, :, :]).then_inc(out_w, 16)

            def load_expert(e):
                sp.dma_start(W1[:, e % 2, :, :], w1[e]).then_inc(w1_ld[e % 2], 16)
                sp.dma_start(W2b[:, e % 2, :], w2[e]).then_inc(w2_ld[e % 2], 16)

            def output_way(b, n, g, kt, place):
                u = NCH * b + n
                G = NG * u + g
                if (kt, place) == (0, 1):
                    sp.wait_ge(o_ev, G + 1)
                    sp.dma_start(o_scr[bass.ds(u, 1), g].rearrange("o p t -> (o p) t"), O[:, g % 2, :]).then_inc(o_w, 16)
                if (kt, place) == (1, 1):
                    wait_apart(sp, (o_w, 16 * (G + 1)))
                    for j in range(HG):
                        r = 32 * j + HD
                        sp.dma_start(sums_c[32 * j:32 * (j + 1), :],
                                     o_scr[bass.ds(u, 1), g, r:r + 1, :].rearrange("o h (j t) -> (o h j) t", t=16)).then_inc(sum_r, 16)
                    if g == 0 and (looped(u) or u >= 1):
                        wait_apart(sp, (x1_s, 2 * u))
                    for j in range(HG):
                        r = 64 * (g % 2) + HD * j
                        sp.dma_start(Op[r:r + HD, g // 2, :],
                                     o_scr[bass.ds(u, 1), g, 32 * j:32 * j + HD, :].rearrange("o p t -> (o p) t")).then_inc(o_r, 16)
                if (kt, place) == (3, 0):
                    sp.wait_ge(rec_s, G + 1)
                    sp.dma_start(rec_scr[bass.ds(u, 1), g].rearrange("o h (j t) -> (o h j) t", t=16), rec_c[:, :]).then_inc(rec_w, 16)
                if (kt, place) == (4, 0):
                    wait_apart(sp, (rec_w, 16 * (G + 1)))
                    if g % 2 == 0 and (looped(u) or u >= 1 or g):
                        wait_apart(sp, (on_s, 2 * u + g // 2))
                    for j in range(HG):
                        r = 64 * (g % 2) + HD * j
                        sp.dma_start(rec_b[r:r + HD, :],
                                     rec_scr[bass.ds(u, 1), g, j:j + 1, :].rearrange("o h t -> (o h) t").to_broadcast([HD, C])
                                     ).then_inc(rec_r, 16)

            def attend(b, n, s, prep, aside, place=None):
                g, kt = divmod(s, KT)
                for pl in range(2) if place is None else (place,):
                    if not (isinstance(b, int) and b == 0 and n == 0 and g == 0) and s < STEPS:
                        if g:
                            output_way(b, n, g - 1, kt, pl) if b is not B or g == 0 else None
                        elif n:
                            output_way(b, 0, NG - 1, kt, pl)
                        else:
                            output_way(b - 1, NCH - 1, NG - 1, kt, pl)
                    if aside is not None:
                        aside(pl)
                if aside is not None and kt == KT - 1:
                    done = 2 * KT * (NG * (NCH * b + n) + g + 1)
                    if g < 2 or n == 0:
                        sp.wait_ge(s_done, done)
                        stack(b, n if g < 2 else n + 1, (g + 2) % NG, st_ld[g % 2], True)
                    elif prep:
                        wait_apart(sp, (s_done, done), (scr_w[0], 64 * (b + 2)), (scr_w[1], 64 * (b + 2)), (flag_s, b + 2))
                        with sp.If(flag_of(b + 1) < 1):
                            stack(b + 1, 0, g - 2, st_ld[g % 2], True)

            def start():
                for slot in range(2):
                    load_expert(slot)

            def turn(b):
                wait_apart(sp, (scr_w[0], 64 * (b + 1)), (scr_w[1], 64 * (b + 1)), (flag_s, b + 1), (m_zero, 16 * B))
                with sp.If(flag_of(b) > 0):
                    if not (isinstance(b, int) and b == 0):
                        wait_apart(sp, (s_done, NCH * PAIRS * b))
                    for n in range(NCH):
                        for g in range(NG):
                            if g >= 2 or n:
                                wait_apart(sp, (ex_mm, 128 * b + 16 * (NG * n + g - 1)))
                            stack(b, n, g, ex_ld[g % 2], False)
                    wait_apart(sp, (m_set, 2 * (b + 1)))
                    sp.dma_start(m_scr[b].rearrange("r h t -> h r t"), Mt[:, :, :]).then_inc(m_w, 16)
                    wait_apart(sp, (m_w, 16 * (b + 1)))
                    stack(b, 0, 0, st_ld[0], True)
                    stack(b, 0, 1, st_ld[1], True)
                with sp.If(flag_of(b) < 1):
                    for slot in range(2):
                        sp.sem_inc(ex_ld[slot], 4 * EX_STACK)
                    sp.sem_inc(m_w, 16)
                    if isinstance(b, int) and b == 0:
                        stack(b, 0, 0, st_ld[0], True)
                        stack(b, 0, 1, st_ld[1], True)

            for dst, src in loads:
                sp.dma_start(dst, src).then_inc(c_ld, 16)
            sp.wait_ge(c_set, N_CONST_SET)
            for b in range(B):
                sp.dma_start(m_scr[b].rearrange("r h t -> h r t"), Mt[:, :, :]).then_inc(m_zero, 16)
            run(sp, Beside(), stage, attend, start, turn)
            for slot in range(2):
                sp.wait_ge(w1_ld[slot], 16 * (4 * B * NCH + 1))
                sp.wait_ge(w2_ld[slot], 16 * (4 * B * NCH + 1))
            sp.wait_ge(out_w, 16 * B * NCH)

        @block.tensor
        def _(pe):
            mm = nc.tensor.matmul

            def read_of(st, a, u):
                return {"xT": (xnT_s, 2 * u + a + 1), "qk": (qk_b, 4 * u + a + 1), "length": (nrm_red, 4 * u + a + 1),
                        "v": (vn_s, 2 * u + a + 1), "wo": (x1_s, 2 * u + a + 1), "nfT": (nfT_s, u + 1),
                        "logits": (gating, GATING * u + 1), "combT": (combT_s, u + 1), "b2": (acc_s, 2 * u + a + 1)}[st]

            def stage(st, a, bb, n, filling):
                k = filling[0]
                u = NCH * bb + n
                if st in FILLS and filling[1]:
                    pe.wait_ge(*read_of(*filling[1]))
                if st == "xT":
                    pe.wait_ge(xn_s, TC * (u + 1))
                    for t in range(TC):
                        last = nc.tensor.transpose(D[:, P * t:P * (t + 1)], xn[:, t, P * a:P * (a + 1)], ident[:, :])
                    last.then_inc(d_full, 1)
                elif st == "qk":
                    pe.wait_ge(xnT_s, 2 * (u + 1))
                    for c in range(CT):
                        last = mm(D[:, :], wqk_sb[:, c, P * a:P * (a + 1)], xnT[:, c, :], start=c == 0, stop=c == CT - 1)
                    last.then_inc(d_full, 1)
                elif st == "length":
                    pe.wait_ge(qk_sq, 4 * u + a + 1)
                    mm(D[:, :], same_head[:, :], sq[:, :], start=True, stop=True).then_inc(d_full, 1)
                elif st == "v":
                    for t in range(2):
                        for c in range(CT):
                            last = mm(D[:, E * t:E * (t + 1)], xnT[:, c, P * (2 * a + t):P * (2 * a + t + 1)], wv_sb[:, c, :],
                                      start=c == 0, stop=c == CT - 1)
                    last.then_inc(d_full, 1)
                elif st == "wo":
                    pe.wait_ge(on_s, 2 * (u + 1))
                    for t in range(2):
                        tok = P * (2 * a + t)
                        for c in range(CT):
                            last = mm(D[:, E * t:E * (t + 1)], Op[:, c, tok:tok + P], wo_sb[:, c, :],
                                      start=c == 0, stop=c == CT - 1)
                    last.then_inc(d_full, 1)
                elif st == "nfT":
                    pe.wait_ge(nf_s, TC * (u + 1))
                    for c in range(CT):
                        for t in range(TC):
                            last = nc.tensor.transpose(D[:, :].bitcast(BF16)[:, C * c + P * t:C * c + P * (t + 1)],
                                                       nf[:, t, P * c:P * (c + 1)], identb[:, :])
                    last.then_inc(d_full, 1)
                elif st == "logits":
                    pe.wait_ge(nfT_s, u + 1)
                    for t in range(TC):
                        for c in range(CT):
                            last = mm(D[:, NE * t:NE * (t + 1)], nfT[:, c, P * t:P * (t + 1)], gate_sb[:, c, :],
                                      start=c == 0, stop=c == CT - 1)
                    last.then_inc(d_full, 1)
                elif st == "combT":
                    pe.wait_ge(comb_s, 3 * (u + 1))
                    for t in range(TC):
                        last = nc.tensor.transpose(D[0:NE, P * t:P * (t + 1)], comb[:, t, :], ident[:, :])
                    last.then_inc(d_full, 1)
                elif st == "b2":
                    pe.wait_ge(combT_s, u + 1)
                    for t in range(2):
                        tok = P * (2 * a + t)
                        last = mm(D[:, E * t:E * (t + 1)], combT[:, tok:tok + P], b2f[:, :], start=True, stop=True)
                    last.then_inc(d_full, 1)
                elif st == "up":
                    expert_up(a, u)
                elif st == "down":
                    expert_down(a, u)

            def expert_up(f, u):
                e, it = divmod(f, 2)
                if it == 0:
                    pe.wait_ge(w1_ld[e % 2], 16 * (4 * u + e // 2 + 1))
                if f == 0:
                    pe.wait_ge(nfT_s, u + 1)
                if f >= LAG:
                    pe.wait_ge(m2_ev, 2 * (NF * u + f - LAG + 1))
                elif f:
                    pe.wait_ge(g_s, NF * u + f)
                for gl, bank in ((0, A), (1, BB)):
                    if gl and f:
                        pe.wait_ge(l_s, NF * u + f)
                    for c in range(CT):
                        last = mm(bank[:, :], W1[:, e % 2, c, FI * gl + P * it:FI * gl + P * (it + 1)], nfT[:, c, :],
                                  start=c == 0, stop=c == CT - 1)
                    last.then_inc(m1_mm, 1)

            def expert_down(m, u):
                e, hh = divmod(m, 2)
                if hh == 0:
                    pe.wait_ge(lo_s, NF * u + m + 2)
                    pe.wait_ge(w2_s, NE * u + e + 1)
                if m + LAG <= NF:
                    pe.wait_ge(g_s, NF * u + m + LAG)
                else:
                    pe.wait_ge(m2_ev, 2 * (NF * u + m))
                for q in range(2):
                    tok = P * (2 * hh + q)
                    for k in range(4):
                        it, part = k // 2, (act_hi, act_lo)[k % 2]
                        last = mm(A[:, E * q:E * (q + 1)], part[:, e % 2, it, tok:tok + P], W2[:, e % 2, E * it:E * (it + 1)],
                                  start=k == 0, stop=k == 3)
                last.then_inc(m2_mm, 1)

            def scores(b, n, s, j2):
                g, kt = divmod(s, KT)
                u = NCH * b + n
                if j2 == 0 and kt == 0:
                    pe.wait_ge(st_ld[g % 2], STACK * (2 * u + g // 2 + 1))
                if s or n or looped(b) or b:
                    pe.wait_ge(exp_done, PAIRS * u + 2 * s + j2 - 1)
                for i in range(2):
                    j = 2 * j2 + i
                    last = mm(S[:, j2, C * i:C * (i + 1)], Ks[0:SROWS + MROWS, g % 2, j, P * kt:P * (kt + 1)],
                              Qs[0:SROWS + MROWS, g % 2, j, :], start=True, stop=True)
                last.then_inc(s_done, 1)

            def values(b, n, s):
                g, kt = divmod(s, KT)
                u = NCH * b + n
                pe.wait_ge(exp_done, PAIRS * u + 2 * (s + 1))
                if n == 0 and g == 0:
                    pe.wait_ge(v_s, KT * b + kt + 1)
                if kt == 0 and (g or n or looped(b) or b):
                    pe.wait_ge(o_ev, NG * u + g)
                for j in range(HG):
                    last = mm(OP[32 * j:32 * j + VW, :], V[:, kt, HG * g + j, :], probs[:, s % 2, C * j:C * (j + 1)],
                              start=kt == 0, stop=kt == KT - 1)
                last.then_inc(av_done, 1)

            def attend(b, n, s, prep, aside, place=None):
                if aside is None:
                    return
                after = (b, n, s + 1) if s + 1 < STEPS else (b, n + 1, 0) if n + 1 < NCH else None
                if after:
                    scores(*after, 0)
                aside(0)
                if after:
                    scores(*after, 1)
                values(b, n, s)
                aside(1)

            def turn(b):
                wait_apart(pe, (flag_s, b + 1))
                flag = pe.value_load(exact_flag[0:1, bass.ds(b, 1)], min_val=0, max_val=1)
                with pe.If(flag > 0):
                    if not (isinstance(b, int) and b == 0):
                        wait_apart(pe, (exp_done, NCH * PAIRS * b))
                    for n in range(NCH):
                        for g in range(NG):
                            wait_apart(pe, (ex_ld[g % 2], EX_STACK * (4 * b + 2 * n + g // 2 + 1)))
                            for j in range(HG):
                                for t in range(TC):
                                    i = 16 * (NG * n + g) + TC * j + t
                                    if i >= 2:
                                        wait_apart(pe, (ex_red, 128 * b + i - 1))
                                    for hf in range(2):
                                        last = mm(S[:, i % 2, C * hf:C * (hf + 1)], Qs[0:SROWS, g % 2, j, P * t:P * (t + 1)],
                                                  Ks[0:SROWS, g % 2, j, C * hf:C * (hf + 1)], start=True, stop=True)
                                    last.then_inc(ex_mm, 1)
                    wait_apart(pe, (ex_red, 128 * (b + 1)))
                    for t in range(TT):
                        last = nc.tensor.transpose(S[0:H, 0, P * t:P * (t + 1)], mx[:, t, :], ident[:, :])
                    last.then_inc(ex_t, 1)
                    wait_apart(pe, (m_set, 2 * (b + 1)))
                with pe.If(flag < 1):
                    pe.sem_inc(ex_mm, 128)
                    pe.sem_inc(ex_t, 1)
                scores(b, 0, 0, 0)
                scores(b, 0, 0, 1)

            pe.wait_ge(c_ld, 16 * N_LOADS)
            pe.wait_ge(c_set, N_CONST_SET)
            run(pe, Beside(), stage, attend, lambda: None, turn)

        @block.scalar
        def _(act):
            def stage(st, a, bb, n, filling):
                k = filling[0]
                u = NCH * bb + n
                if st == "xT" and a == 0:
                    act.wait_ge(d_full, k + 1)
                    nc.scalar.copy(xnT[:, 0, :], D[:, :]).then_inc(xnT_s, 1)
                elif st == "qk":
                    act.wait_ge(d_full, k + 1)
                    if looped(u) or u or a >= 2:
                        act.wait_ge(qk_sw, 4 * u + a - 1)
                        act.wait_ge(qk_cos, 4 * u + a - 1)
                    nc.scalar.activation(qb[:, a % 2, :], D[:, :], ACT.Identity, bias=bqk_sb[:, a:a + 1]).then_inc(qk_b, 1)
                elif st == "part1":
                    act.wait_ge(qk_rot, 4 * u + a + 1)
                    if looped(u) or u or a >= 2:
                        act.wait_ge(scr_w[a % 2], 32 * u + 16 * (a // 2))
                    nc.scalar.copy(parts[:, a % 2, 0, :], rot[:, a % 2, :]).then_inc(qk_p1, 1)
                    if looped(u) or u or a:
                        act.wait_ge(nrm_red, 4 * u + a)
                    nc.scalar.activation(sq[:, :], rot[:, a % 2, :], ACT.Square).then_inc(qk_sq, 1)
                elif st == "part2":
                    act.wait_ge(qk_r1, 4 * u + a + 1)
                    nc.scalar.copy(parts[:, a % 2, 1, :], sw[:, a % 2, :]).then_inc(qk_p2, 1)
                elif st == "ss":
                    for t in range(TC):
                        act.wait_ge(xc_s, TC * u + t + 1)
                        if t:
                            act.wait_ge(ss_s, TC * u + t)
                        nc.scalar.activation(sqs[:, :], xc[:, n, t, :], ACT.Square, accum_out=ss[:, t:t + 1]).then_inc(ss_s, 1)
                elif st == "nfT":
                    act.wait_ge(d_full, k + 1)
                    nc.scalar.copy(nfT[:, :, :].rearrange("p c t -> p (c t)"), D[:, :].bitcast(BF16)).then_inc(nfT_s, 1)
                elif st == "etop":
                    act.wait_ge(dtop_s, u + 1)
                    nc.scalar.activation(etop[:, :], dtop[:, :], ACT.Exp).then_inc(etop_s, 1)
                elif st == "tanh":
                    act.wait_ge(g_s, NF * u + a + 1)
                    if looped(u) or u or a >= 2:
                        act.wait_ge(act_s, NF * u + a - 1)
                    nc.scalar.activation(th_sb[:, a % 2, :], g_sb[:, a % 2, :], ACT.Tanh, scale=ALPHA / 2).then_inc(th_s, 1)

            def exps(b, n, s, j2):
                u = NCH * b + n
                act.wait_ge(s_done, PAIRS * u + 2 * s + j2 + 1)
                if j2 == 0 and (s >= 2 or n or looped(b) or b):
                    act.wait_ge(av_done, STEPS * u + s - 1)
                nc.scalar.activation(probs[:, s % 2, 2 * C * j2:2 * C * (j2 + 1)], S[:, j2, :], ACT.Exp,
                                     scale=SCALE).then_inc(exp_done, 1)

            def attend(b, n, s, prep, aside, place=None):
                if aside is None:
                    return
                if n == 0 and s == 0:
                    exps(b, 0, 0, 0)
                    exps(b, 0, 0, 1)
                after = (b, n, s + 1) if s + 1 < STEPS else (b, n + 1, 0) if n + 1 < NCH else None
                if after:
                    exps(*after, 0)
                aside(0)
                if after:
                    exps(*after, 1)
                aside(1)

            act.wait_ge(c_ld, 16 * N_LOADS)
            run(act, Beside(), stage, attend, lambda: None, lambda b: None)

        @block.gpsimd
        def _(pool):
            tt = nc.gpsimd.tensor_tensor

            def stage(st, a, bb, n, filling):
                k = filling[0]
                u = NCH * bb + n
                if st == "rstd1":
                    pool.wait_ge(var1_s, u + 1)
                    tt(rstd1[:, :], var1[:, :], half_pow[:, :], ALU.pow).then_inc(rstd1_s, 1)
                elif st == "rope":
                    cols, q = slice(C * n, C * (n + 1)), a % 2
                    pool.wait_ge(qk_b, 4 * u + a + 1)
                    if looped(u) or u or a >= 2:
                        pool.wait_ge(qk_r1, 4 * u + a - 1)
                        pool.wait_ge(qk_sq, 4 * u + a - 1)
                    tt(rot[:, q, :], qb[:, q, :], cos_sb[:, cols], ALU.mult).then_inc(qk_cos, 1)
                    pool.wait_ge(qk_sw, 4 * u + a + 1)
                    tt(sw[:, q, :], sw[:, q, :], sin_sb[:, cols], ALU.mult).then_inc(qk_sin, 1)
                    pool.wait_ge(qk_cos, 4 * u + a + 1)
                    pool.wait_ge(qk_sin, 4 * u + a + 1)
                    tt(rot[:, q, :], rot[:, q, :], sw[:, q, :], ALU.add).then_inc(qk_rot, 1)
                elif st == "length":
                    pool.wait_ge(qk_p1, 4 * u + a + 1)
                    tt(sw[:, a % 2, :], rot[:, a % 2, :], parts[:, a % 2, 0, :], ALU.subtract).then_inc(qk_r1, 1)
                elif st == "guard" and n == NCH - 1:
                    wait_apart(pool, (nsq_s, bb + 1))
                    nc.gpsimd.partition_all_reduce(nsqa[:, :], nsq2[:, :], P, bass.bass_isa.ReduceOp.max).then_inc(nsqa_s, 1)
                elif st == "x1_b":
                    wait_apart(pool, (x1_ld, 16 * (u + 1)))
                    tt(X1s[:, n, :, :], X1s[:, n, :, :], bo_sb[:, None, :].to_broadcast([P, TC, E]), ALU.add).then_inc(x1_b, 1)
                elif st == "rstd2":
                    pool.wait_ge(var2_s, u + 1)
                    tt(rstd2[:, :], var2[:, :], half_pow[:, :], ALU.pow).then_inc(rstd2_s, 1)
                elif st == "rrms":
                    pool.wait_ge(ms_s, u + 1)
                    tt(rrms[:, :], ms[:, :], half_pow[:, :], ALU.pow).then_inc(rrms_s, 1)
                elif st == "hidden":
                    e, it = divmod(a, 2)
                    if it == 0:
                        wait_apart(pool, (w2_ld[e % 2], 16 * (4 * u + e // 2 + 1)))
                        if looped(u) or u or e >= 2:
                            wait_apart(pool, (m2_mm, NF * u + 2 * (e - 1)))
                        nc.gpsimd.tensor_scalar(W2[:, e % 2, :], W2b[:, e % 2, :], 1.0, 1.0, ALU.mult, ALU.mult).then_inc(w2_s, 1)
                    if looped(u) or u or e >= 2:
                        pool.wait_ge(m2_mm, NF * u + 2 * (e - 1))
                    pool.wait_ge(hi_s, NF * u + a + 1)
                    tt(act_lo[:, e % 2, it, :], act_sb[:, a % 2, :], act_hi[:, e % 2, it, :].bitcast(FP32),
                       ALU.subtract).then_inc(lo_s, 1)

            def attend(b, n, s, prep, aside, place=None):
                g, kt = divmod(s, KT)
                if kt == 5 and place in (None, 0) and g % 2 == 0 and s < STEPS \
                        and not (isinstance(b, int) and b == 0 and n == 0 and g == 0):
                    u, c = (NCH * b + n, 0) if g else (NCH * b + n - 1, 1)
                    if b is not B or g == 0:
                        pool.wait_ge(rec_r, 64 * (NG * u + 2 * (c + 1)))
                        pool.wait_ge(o_r, 64 * (NG * u + 2 * (c + 1)))
                        tt(Op[:, c, :], Op[:, c, :], rec_b[:, :], ALU.mult).then_inc(on_s, 1)
                if aside is not None:
                    aside(0)
                    aside(1)

            pool.wait_ge(c_ld, 16 * N_LOADS)
            pool.wait_ge(c_set, N_CONST_SET)
            run(pool, Beside(), stage, attend, lambda: None, lambda b: None)

        @block.vector
        def _(dve):
            v = nc.vector

            def norm_stats(src, st, mv, var, stat_s, aggr_s, var_s, u):
                for t in range(TC):
                    v.bn_stats(st[:, t, :], src[:, t, :]).then_inc(stat_s, 1)
                for t in range(TC):
                    wait_apart(dve, (stat_s, TC * u + t + 1))
                    v.bn_aggr(mv[:, t, :], st[:, t, :]).then_inc(aggr_s, 1)
                dve.wait_ge(aggr_s, TC * (u + 1))
                v.tensor_scalar(var[:, :], mv[:, :, 1], EPS, None, ALU.add).then_inc(var_s, 1)

            def stage(st, a, bb, n, filling):
                k = filling[0]
                u = NCH * bb + n
                if st == "stats1":
                    dve.wait_ge(x_ld, 16 * (u + 1))
                    norm_stats(X, st1, mv1, var1, stat1, aggr1, var1_s, u)
                elif st == "xn":
                    dve.wait_ge(rstd1_s, u + 1)
                    for t in range(TC):
                        v.tensor_scalar(xn[:, t, :], X[:, t, :], mv1[:, t, 0:1], rstd1[:, t:t + 1],
                                        ALU.subtract, ALU.mult).then_inc(xn_s, 1)
                elif st == "xT" and a == 1:
                    dve.wait_ge(d_full, k + 1)
                    v.tensor_copy(xnT[:, 1, :], D[:, :]).then_inc(xnT_s, 1)
                elif st == "rope":
                    wait_apart(dve, (qk_b, 4 * u + a + 1), *([(qk_p3, 4 * u + a - 1)] if looped(u) or u or a >= 2 else []))
                    v.stream_shuffle(sw[:, a % 2, :], qb[:, a % 2, :], [r ^ 1 for r in range(32)]).then_inc(qk_sw, 1)
                elif st == "part3":
                    dve.wait_ge(qk_p2, 4 * u + a + 1)
                    v.tensor_tensor(parts[:, a % 2, 2, :], sw[:, a % 2, :], parts[:, a % 2, 1, :], ALU.subtract).then_inc(qk_p3, 1)
                elif st == "length":
                    t, hf = divmod(a, 2)
                    dve.wait_ge(d_full, k + 1)
                    v.reduce_max(nsq[:, t, 2 * hf + n:2 * hf + n + 1], D[:, :], AX_X).then_inc(nrm_red, 1)
                elif st == "guard" and n == NCH - 1:
                    v.reduce_max(nsq2[:, :], nsq[:, :, :], AX_X).then_inc(nsq_s, 1)
                    dve.wait_ge(nsqa_s, bb + 1)
                    v.tensor_tensor(bound[:, :], nsqa[:, 0:1], nsqa[:, 1:2], ALU.mult).then_inc(bound_s, 1)
                    dve.wait_ge(bound_s, bb + 1)
                    v.tensor_scalar(exact_flag[:, bass.ds(bb, 1)], bound[:, :],
                                    (safe_score / SCALE) ** 2 / 1.05 if safe_score > 0 else -1.0, None, ALU.is_gt).then_inc(flag_s, 1)
                elif st == "v":
                    if n == 0 and a == 0 and (looped(bb) or bb):
                        dve.wait_ge(v_s, KT * bb)
                    dve.wait_ge(d_full, k + 1)
                    t = TC * n + 2 * a
                    v.tensor_tensor(Vn[:, t:t + 2, :, :], D[:, :].rearrange("p (t h d) -> p t h d", t=2, h=H),
                                    bv_sb[:, :].rearrange("p (h d) -> p h d", h=H)[:, None, :, :].to_broadcast([P, 2, H, HD]),
                                    ALU.add).then_inc(vn_s, 1)
                elif st == "wo":
                    dve.wait_ge(x1_b, u + 1)
                    dve.wait_ge(d_full, k + 1)
                    xh = X1s[:, n, 2 * a:2 * a + 2, :].rearrange("p t c -> p (t c)")
                    v.tensor_tensor(xh, D[:, :], xh, ALU.add).then_inc(x1_s, 1)
                elif st == "stats2":
                    dve.wait_ge(x1_s, 2 * (u + 1))
                    norm_stats(X1s[:, n], st2, mv2, var2, stat2, aggr2, var2_s, u)
                elif st == "xc":
                    dve.wait_ge(rstd2_s, u + 1)
                    for t in range(TC):
                        v.tensor_scalar(xc[:, n, t, :], X1s[:, n, t, :], mv2[:, t, 0:1], rstd2[:, t:t + 1],
                                        ALU.subtract, ALU.mult).then_inc(xc_s, 1)
                elif st == "ms":
                    dve.wait_ge(ss_s, TC * (u + 1))
                    v.tensor_scalar(ms[:, :], ss[:, :], 1.0 / E, EPS, ALU.mult, ALU.add).then_inc(ms_s, 1)
                elif st == "nf":
                    dve.wait_ge(rrms_s, u + 1)
                    for t in range(TC):
                        v.scalar_tensor_tensor(nf[:, t, :], xc[:, n, t, :], rrms[:, t:t + 1], nw_sb[:, :],
                                               ALU.mult, ALU.mult).then_inc(nf_s, 1)
                elif st == "logits":
                    dve.wait_ge(d_full, k + 1)
                    v.tensor_tensor(lgb[:, :, :], D[:, 0:TC * NE].rearrange("p (t e) -> p t e", e=NE),
                                    gate_b_sb[:, None, :].to_broadcast([P, TC, NE]), ALU.add).then_inc(gating, 1)
                elif st == "gates1":
                    gates1(u)
                elif st == "gates2":
                    gates2(u)
                elif st == "combT":
                    dve.wait_ge(d_full, k + 1)
                    v.tensor_copy(combT[:, :], D[0:NE, :]).then_inc(combT_s, 1)
                elif st == "b2":
                    dve.wait_ge(d_full, k + 1)
                    if looped(u) or u:
                        dve.wait_ge(out_w, 16 * u)
                    v.tensor_copy(acc[:, 2 * a:2 * a + 2, :].rearrange("p t c -> p (t c)"), D[:, :]).then_inc(acc_s, 1)
                elif st in ("up", "hidden", "down"):
                    expert(st, a, u)
                elif st == "final":
                    final(u, n)

            def chain(u, k):
                done = [k]

                def link(ins):
                    done[0] += 1
                    ins.then_inc(gating, 1)
                    dve.wait_ge(gating, GATING * u + done[0])
                    return done[0]
                return link

            def over_experts(x):
                return x[:, :, None].to_broadcast([P, TC, NE])

            def gates1(u):
                link = chain(u, 1)

                def first_of(onehot, logits, top):
                    link(v.reduce_max(top[:, :], logits, AX_X))
                    link(v.tensor_tensor(pick[:, :, :], logits, over_experts(top), ALU.is_equal))
                    link(v.tensor_tensor(pick[:, :, :], pick[:, :, :], rank[:, None, :].to_broadcast([P, TC, NE]), ALU.mult))
                    link(v.reduce_max(pickm[:, :], pick[:, :, :], AX_X))
                    return link(v.tensor_tensor(onehot[:, :, :], pick[:, :, :], over_experts(pickm), ALU.is_equal))

                dve.wait_ge(gating, GATING * u + 1)
                link(v.tensor_copy(lgt[:, :, :], lgb[:, :, :]))
                first_of(oh1, lgt[:, :, :], top1)
                link(v.scalar_tensor_tensor(lg2[:, :, :], oh1[:, :, :], -3.0e38, lgt[:, :, :], ALU.mult, ALU.add))
                assert first_of(oh2, lg2[:, :, :], top2) == GATES1
                v.tensor_tensor(dtop[:, :], top2[:, :], top1[:, :], ALU.subtract).then_inc(dtop_s, 1)

            def gates2(u):
                link = chain(u, GATES1)
                dve.wait_ge(etop_s, u + 1)
                link(v.tensor_scalar(w_2[:, :], etop[:, :], 1.0, None, ALU.add))
                link(v.reciprocal(w_1[:, :], w_2[:, :]))
                link(v.tensor_tensor(w_2[:, :], w_1[:, :], etop[:, :], ALU.mult))
                link(v.tensor_tensor(oh1[:, :, :], oh1[:, :, :], over_experts(w_1), ALU.mult))
                assert link(v.tensor_tensor(oh2[:, :, :], oh2[:, :, :], over_experts(w_2), ALU.mult)) == GATING
                v.tensor_tensor(comb[:, :, :], oh1[:, :, :], oh2[:, :, :], ALU.add).then_inc(comb_s, 1)
                dve.wait_ge(comb_s, 3 * u + 1)
                v.tensor_scalar(combh[:, :, :], comb[:, :, :], 0.5, None, ALU.mult).then_inc(comb_s, 2)

            def expert(st, f, u):
                e, it = divmod(f, 2)
                q, n = f % 2, NF * u + f
                if st == "up":
                    dve.wait_ge(m1_mm, 2 * n + 1)
                    if looped(u) or u or f >= 2:
                        dve.wait_ge(act_s, n - 1)
                    v.tensor_scalar(g_sb[:, q, :], A[:, :], b1f[:, e, 0, it:it + 1], LIMIT, ALU.add, ALU.min).then_inc(g_s, 1)
                    dve.wait_ge(m1_mm, 2 * n + 2)
                    v.tensor_scalar(l_sb[:, q, :], BB[:, :], b1f[:, e, 1, it:it + 1], 1.0 - LIMIT, ALU.add, ALU.max).then_inc(l_s, 1)
                if st == "down":
                    dve.wait_ge(m2_mm, n + 1)
                    if f == 0:
                        dve.wait_ge(acc_s, 2 * (u + 1))
                    else:
                        dve.wait_ge(m2_ev, 2 * n)
                    for i in range(2):
                        t = 2 * it + i
                        v.scalar_tensor_tensor(acc[:, t, :], A[:, E * i:E * (i + 1)], combh[:, t, e:e + 1], acc[:, t, :],
                                               ALU.mult, ALU.add).then_inc(m2_ev, 1)
                if st == "hidden":
                    dve.wait_ge(th_s, n + 1)
                    v.scalar_tensor_tensor(th_sb[:, q, :], th_sb[:, q, :], 1.0, g_sb[:, q, :], ALU.add, ALU.mult).then_inc(t1_s, 1)
                    dve.wait_ge(t1_s, n + 1)
                    dve.wait_ge(l_s, n + 1)
                    if looped(u) or u or f >= 2:
                        dve.wait_ge(lo_s, n - 1)
                    v.scalar_tensor_tensor(act_sb[:, q, :], l_sb[:, q, :], 1.0 + LIMIT, th_sb[:, q, :],
                                           ALU.min, ALU.mult).then_inc(act_s, 1)
                    dve.wait_ge(act_s, n + 1)
                    if looped(u) or u or e >= 2:
                        dve.wait_ge(m2_mm, NF * u + 2 * (e - 1))
                    v.tensor_copy(act_hi[:, e % 2, it, :], act_sb[:, q, :]).then_inc(hi_s, 1)

            def final(u, n):
                accv, x1v = (t[:, :, :].rearrange("p t c -> p (t c)") for t in (acc, X1s[:, n]))
                cb, xcv = (t[:, :, :].rearrange("p t c -> p (t c)") for t in (x2b, xc[:, n]))
                dve.wait_ge(m2_ev, 2 * NF * (u + 1))
                v.tensor_copy(cb, accv).then_inc(cb_s, 1)
                dve.wait_ge(cb_s, u + 1)
                v.tensor_tensor(cb, cb, xcv, ALU.add).then_inc(fo_s, 1)
                dve.wait_ge(fo_s, u + 1)
                for hf in range(2):
                    r = slice(C * hf, C * (hf + 1))
                    v.tensor_tensor(accv[:, r], x1v[:, r], cb[:, r], ALU.add).then_inc(x2_s, 1)

            def move_v(b, kt):
                if looped(b) or b >= 0:
                    dve.wait_ge(av_done, NCH * STEPS * b + NCH * STEPS - KT + kt + 1)
                dve.wait_ge(vn_s, 4 * (b + 2))
                v.tensor_copy(V[:, kt, :, 0:HD], Vn[:, kt, :, :]).then_inc(v_s, 1)

            def attend(b, n, s, prep, aside, place=None):
                g, kt = divmod(s, KT)
                first = isinstance(b, int) and b == 0 and n == 0 and g == 0
                if b is not B or g == 0:
                    G = NG * (NCH * b + n) + g - 1
                    if kt == 0 and not first and place in (None, 0):
                        dve.wait_ge(av_done, KT * (G + 1))
                        if G if isinstance(G, int) else True:
                            if looped(G) or G >= 2:
                                dve.wait_ge(o_w, 16 * (G - 1))
                        v.tensor_copy(O[:, (g - 1) % 2, :], OP[:, :]).then_inc(o_ev, 1)
                    if kt == 3 and not first and place in (None, 0):
                        dve.wait_ge(sum_r, 64 * (G + 1))
                        v.reciprocal(rec_c[:, :], sums_c[:, :]).then_inc(rec_s, 1)
                if aside is not None:
                    if n == NCH - 1 and g == NG - 1 and kt and prep:
                        move_v(b, kt - 1)
                    aside(0)
                    aside(1)

            def turn(b):
                move_v(b - 1, KT - 1) if looped(b) or b else [move_v(-1, kt) for kt in range(KT)]
                wait_apart(dve, (flag_s, b + 1))
                flag = dve.value_load(exact_flag[0:1, bass.ds(b, 1)], min_val=0, max_val=1)
                with dve.If(flag > 0):
                    for i in range(128):
                        n, g, j, t = i // 64, i // 16 % NG, i // TC % HG, i % TC
                        wait_apart(dve, (ex_mm, 128 * b + i + 1))
                        h = HG * g + j
                        v.reduce_max(mx[:, TC * n + t, h:h + 1], S[:, i % 2, :], AX_X).then_inc(ex_red, 1)
                    wait_apart(dve, (ex_t, b + 1))
                    if not (isinstance(b, int) and b == 0):
                        wait_apart(dve, (m_w, 16 * b))
                    v.tensor_scalar(Mt[:, 0, :], S[0:H, 0, :], -1.0, None, ALU.mult).then_inc(m_set, 1)
                    wait_apart(dve, (m_set, 2 * b + 1))
                    v.scalar_tensor_tensor(Mt[:, 1, :], S[0:H, 0, :], -1.0, Mt[:, 0, :], ALU.mult, ALU.subtract).then_inc(m_set, 1)
                with dve.If(flag < 1):
                    dve.sem_inc(m_set, 2)
                    dve.sem_inc(ex_red, 128)

            v.memset(half_pow[:, :], -0.5).then_inc(c_set, 1)
            v.memset(V[:, :, :, HD:VW], 1.0).then_inc(c_set, 1)
            v.memset(Ks[SROWS:SROWS + MROWS, :, :, :], 1.0).then_inc(c_set, 1)
            v.memset(OP[:, :], 0.0).then_inc(c_set, 1)
            v.memset(Mt[:, :, :], 0.0).then_inc(c_set, 1)
            dve.wait_ge(c_ld, 16 * N_LOADS)
            v.tensor_copy(identb[:, :], ident[:, :]).then_inc(c_set, 1)
            v.tensor_copy(same_head[:, :], same_head_f[:, :]).then_inc(c_set, 1)
            v.tensor_copy(b1f[:, :, 0, :], b1_sb[:, :, 0, :]).then_inc(c_set, 1)
            v.tensor_scalar(b1f[:, :, 1, :], b1_sb[:, :, 1, :], 1.0, None, ALU.add).then_inc(c_set, 1)
            v.tensor_copy(b2f[:, :], b2_sb[:, :]).then_inc(c_set, 1)
            dve.wait_ge(c_set, N_CONST_SET)
            run(dve, Beside(), stage, attend, lambda: None, turn)


def layouts(np, d):
    f = lambda n: np.asarray(d[n])
    wq, wk, wv, wo = (f(f"L0_attn_W{n}") for n in "qkvo")
    w1 = f("L0_ffn_mlp1_weight").reshape(NE, CT, P, 2, CT, P)
    w2 = f("L0_ffn_mlp2_weight").reshape(NE, E, CT, P)
    b1 = f("L0_ffn_mlp1_bias").reshape(NE, CT, P, 2)
    return {
        "x": f("L0_attn_x"),
        "wqk": np.concatenate([wq.T, wk.T], axis=1),
        "bqk": np.concatenate([f("L0_attn_bq"), f("L0_attn_bk")]).reshape(4, P).T,
        "wv": wv.T,
        "bv": f("L0_attn_bv"),
        "wo": wo.T,
        "bo": f("L0_attn_bo"),
        "nw": f("L0_ffn_norm_weight"),
        "gate": f("L0_ffn_gate_weight").T,
        "gate_b": f("L0_ffn_gate_bias"),
        "w1": w1.transpose(0, 5, 4, 3, 1, 2).reshape(NE, P, CT, 2 * FI),
        "b1": b1.transpose(2, 0, 3, 1),
        "w2": w2.transpose(0, 3, 2, 1),
        "b2": f("L0_ffn_mlp2_bias"),
    }


def constants(np):
    inv = (1.0 / np.float32(10000.0) ** (np.arange(0, HD, 2, dtype=np.float32) / np.float32(HD))).astype(np.float32)
    ang = (np.arange(L, dtype=np.float32)[:, None] * inv[None, :]).astype(np.float32)
    ang = np.tile(np.repeat(ang, 2, axis=1).T, (P // HD, 1))
    sign = np.where(np.arange(P) % 2 == 0, -1.0, 1.0).astype(np.float32)[:, None]
    head = np.arange(P) // HD
    return {
        "rope": np.stack([np.cos(ang), np.sin(ang) * sign]).astype(np.float32),
        "ident_in": np.eye(P, dtype=np.float32),
        "heads_in": (head[:, None] == head[None, :]).astype(np.float32),
        "rank_in": np.arange(NE, 0, -1).astype(np.float32),
    }


def kernel(**inputs):
    import numpy as _np
    import concourse.bacc as _bacc
    from concourse.bass_utils import run_bass_kernel_spmd as _run

    nc = _bacc.Bacc("TRN2", target_bir_lowering=False, num_devices=1)
    arrays, args = {}, {}
    for name, a in {**layouts(_np, inputs), **constants(_np)}.items():
        a = _np.ascontiguousarray(a)
        arrays[f"in_{name}"] = a
        args[name] = nc.dram_tensor(f"in_{name}", a.shape, mybir.dt.from_np(a.dtype), kind="ExternalInput").ap()
    args["out"] = nc.dram_tensor("out_0", (B, L, E), FP32, kind="ExternalOutput").ap()
    block_kernel(nc, **args)
    r = _run(nc, [arrays], core_ids=[0])
    return r.results[0]["out_0"]
```

```python
from contextlib import ExitStack

import concourse.bass as bass
from concourse import mybir

FP32 = mybir.dt.float32
FP32R = mybir.dt.float32r
BF16 = mybir.dt.bfloat16
INT32 = mybir.dt.int32
ALU = mybir.AluOpType
ACT = mybir.ActivationFunctionType
AX_X = mybir.AxisListType.X

P = 128
B, L, E = 4, 1024, 256
H, HD = 16, 16
NE, TOPK, FI = 8, 2, 256
LIMIT, ALPHA, EPS = 7.0, 1.702, 1e-5
CT = E // P
TT = L // P
HG = 4
NG = H // HG
KT = L // P
STEPS = NG * KT
C = 512
NCH = L // C
TC = C // P
NF = 2 * NE
SROWS = 6 * HD
MROWS = 2
VW = HD + 1
SCALE = HD ** -0.5
SAFE_SCORE = 60.0
PRODUCTS = ((0, 3), (1, 2), (2, 1))


def looped(value):
    return not isinstance(value, int)


def block_kernel(nc, x, wqk, bqk, wv, bv, wo, bo, nw, gate, gate_b, w1, b1, w2, b2, rope, ident_in, heads_in, rank_in, ones_in,
                 out, safe_score=SAFE_SCORE):

    AT = {"x_in": 0, "stats1": 1, "rstd1": 1, "xn": 4, "xT0": 7, "xT1": 8,
          "qk0": 10, "qk1": 12, "qk2": 22, "qk3": 30,
          "rope": 2, "part1": 3, "length": 5, "part2": 7, "part3": 10,
          "v0": 37, "v1": 42, "guard": 1, "flag": 8,
          "x1_in": 0, "x1_b": 7, "wo0": 13, "wo1": 14, "stats2": 15, "rstd2": 16, "xc": 17, "ss": 18, "ms": 18,
          "rrms": 20, "nf": 22, "nfT": 24, "logits": 26, "gates1": 26, "etop": 27, "gates2": 28, "combT": 32,
          "b20": 33, "b21": 34}
    FFN0, LAG = 26, 4
    DOWN, TANH, HIDDEN, UP, LO, W2AT = 0, 2, 2, 1, 5, 3
    PREP = {}
    POST = {}
    EXPERTS = {}

    def half_at(f):
        return f * 3 // 2 * 2

    def place(table, half, *stages):
        table.setdefault(divmod(half, 2), []).extend(stages)

    for st in ("x_in", "stats1", "rstd1", "xn"):
        place(PREP, AT[st], (st, 0))
    for a in range(2):
        place(PREP, AT[f"xT{a}"], ("xT", a))
        place(PREP, AT[f"v{a}"], ("v", a))
    for a in range(4):
        h = AT[f"qk{a}"]
        place(PREP, h, ("qk", a))
        for st in ("rope", "part1", "length", "part2", "part3"):
            place(PREP, h + AT[st], (st, a))
    place(PREP, h + AT["length"] + AT["guard"], ("guard", 0))
    place(PREP, h + AT["length"] + AT["guard"] + AT["flag"], ("flag", 0))

    for st in ("x1_in", "x1_b", "stats2", "rstd2", "xc", "ss", "ms", "rrms", "nf", "nfT", "logits", "gates1", "etop",
               "gates2", "combT"):
        place(POST, AT[st], (st, 0))
    for a in range(2):
        place(POST, AT[f"wo{a}"], ("wo", a))
        place(POST, AT[f"b2{a}"], ("b2", a))

    for f in range(NF + LAG):
        h = FFN0 + half_at(f)
        if f >= LAG:
            place(EXPERTS, h + DOWN, ("down", f - LAG))
        if f < NF:
            place(EXPERTS, h + UP, ("up", f))
    for f in range(NF):
        for st, off in (("tanh", TANH), ("hidden", HIDDEN), ("w2", W2AT), ("lo", LO)):
            place(EXPERTS, FFN0 + half_at(f + 1) + off - 2, (st, f))
    h = FFN0 + half_at(NF + LAG - 1) + 1
    FINAL = h // 2
    place(EXPERTS, h, ("final", 0))
    ORDER = ("down", "tanh", "hidden", "w2", "lo", "up", "final")
    for l in EXPERTS.values():
        l.sort(key=lambda e: (ORDER.index(e[0]), e[1]))

    HEAD = [("stats1", 0, 0), ("rstd1", 0, 0), ("xn", 0, 0), ("x_in", 0, 1), ("early", 0, 0), ("xT", 0, 0), ("xT", 1, 0)]
    for i in range(4 * NCH + 2):
        tile = [(j % 4, j // 4) for j in (i, i - 1, i - 2)]
        if i < 4 * NCH:
            HEAD += [("qk", *tile[0])]
        if i >= 2:
            HEAD += [("length", *tile[2]), ("part2", *tile[2]), ("part3", *tile[2])]
        if i < 4 * NCH:
            HEAD += [("rope", *tile[0])]
        if i == 0:
            HEAD += [("stats1", 0, 1), ("rstd1", 0, 1)]
        if i == 1:
            HEAD += [("xn", 0, 1)]
        if i == 2:
            HEAD += [("weights", 0, 0)]
        if i % 4 == 3:
            HEAD += [("v", 0, i // 4), ("v", 1, i // 4)]
        if i == 3:
            HEAD += [("xT", 0, 1), ("xT", 1, 1)]
        if 1 <= i <= 4 * NCH:
            HEAD += [("part1", *tile[1])]
        if i < 4 * NCH:
            HEAD += [("sum", *tile[0])]
    HEAD += [("guard", 0, 1), ("flag", 0, 1)]
    HEAD_BANKS = 4
    FILLS = ("xT", "qk", "v", "length", "wo", "nfT", "logits", "combT", "b2")
    PREP_FILLS = sum(st in FILLS for l in PREP.values() for st, _ in l)
    POST_FILLS = sum(st in FILLS for l in POST.values() for st, _ in l)

    class Beside:

        def at(self, base, b, n, prep, post):
            self.n, self.last = base, None
            if looped(base) or base:
                for step in range(STEPS):
                    for half in range(2):
                        for _ in self.stages(b, n, step, half, prep, post, False):
                            pass
                self.n = base

        def stages(self, b, n, step, place, prep, post, late):
            todo = []
            after, before, before2 = (b + 1, n), ((b, n - 1) if n else (b - 1, NCH - 1)), (b - 1, n)
            if late:
                todo += [(st, a, before2) for st, a in EXPERTS.get((step + STEPS, place), [])]
            if prep:
                todo += [(st, a, after) for st, a in PREP.get((step, place), [])]
            if post:
                todo += [(st, a, before) for st, a in POST.get((step, place), [])]
                todo += [(st, a, before) for st, a in EXPERTS.get((step, place), [])]
            for st, a, (batch, chunk) in todo:
                k = (self.n, self.last, False)
                if st in FILLS:
                    self.n, self.last = self.n + 1, (st, a, NCH * batch + chunk)
                elif st == "down" and not alone(NCH * batch + chunk):
                    self.last = (st, a, NCH * batch + chunk)
                yield st, a, batch, chunk, k

        def head(self):
            made = []
            for st, a, n in HEAD:
                k = (self.n, made[-HEAD_BANKS] if len(made) >= HEAD_BANKS else None, True)
                if st in FILLS:
                    made.append((st, a, n))
                    self.n, self.last = self.n + 1, made[-1]
                yield st, a, 0, n, k

    ctx = ExitStack()
    with ctx:
        def sb(name, shape, dt):
            return ctx.enter_context(nc.sbuf_tensor(name, shape, dt))

        def ps(name, shape, dt):
            return ctx.enter_context(nc.psum_tensor(name, shape, dt))

        def sem(name):
            return ctx.enter_context(nc.semaphore(name))

        def scratch(name, shape, dt):
            return nc.dram_tensor(name, shape, dt, kind="Internal").ap()

        q_scr = scratch("q_scr", (B, NCH, 3, E, C), BF16)
        k_scr = scratch("k_scr", (B, 3, E, L), BF16)
        m_scr = scratch("m_scr", (B, MROWS, H, L), BF16)
        o_scr = scratch("o_scr", (B * NCH, NG, P, C), FP32)
        rec_scr = scratch("rec_scr", (B * NCH, NG, HG, C), FP32)

        wqk_sb = sb("wqk_sb", [P, CT, 2 * E], FP32)
        bqk_sb = sb("bqk_sb", [P, 4], FP32)
        wv_sb = sb("wv_sb", [P, CT, E], FP32)
        bv_sb = sb("bv_sb", [P, E], FP32)
        wo_sb = sb("wo_sb", [P, CT, E], FP32)
        bo_sb = sb("bo_sb", [P, E], FP32)
        nw_sb = sb("nw_sb", [P, E], FP32)
        gate_sb = sb("gate_sb", [P, CT, NE], BF16)
        gate_b_sb = sb("gate_b_sb", [P, NE], BF16)
        b1_sb = sb("b1_sb", [P, NE, 2, CT], BF16)
        b1f = sb("b1f", [P, NE, 2, CT], FP32)
        b2_sb = sb("b2_sb", [NE, E], BF16)
        b2f = sb("b2f", [NE, E], FP32)
        cos_sb = sb("cos_sb", [P, L], FP32)
        sin_sb = sb("sin_sb", [P, L], FP32)
        ident = sb("ident", [P, P], FP32)
        identb = sb("identb", [P, P], BF16)
        same_head_f = sb("same_head_f", [P, P], FP32)
        same_head = sb("same_head", [P, P], BF16)
        rank = sb("rank", [P, NE], FP32)
        half_pow = sb("half_pow", [P, TC], FP32)

        X = sb("X", [P, TC, E], FP32)
        xn = sb("xn", [P, TC, E], FP32)
        xnT = sb("xnT", [P, CT, C], FP32)
        qb = sb("qb", [P, 2, C], FP32)
        sw = sb("sw", [P, 2, C], FP32)
        rot = sb("rot", [P, 2, C], FP32)
        parts = sb("parts", [P, 2, 3, C], BF16)
        sq = sb("sq", [P, C], BF16)
        Vn = sb("Vn", [P, KT, H, HD], FP32)

        V = sb("V", [P, KT, H, VW], FP32)
        Qs = sb("Qs", [P, 2, HG, C], BF16)
        Ks = sb("Ks", [P, 2, HG, L], BF16)
        probs = sb("probs", [P, 2, HG * C], FP32)
        O = sb("O", [P, 2, C], FP32)
        Op = sb("Op", [P, CT, C], FP32)
        rec_b = sb("rec_b", [P, C], FP32)
        sums_c = sb("sums_c", [P, 16], FP32)
        rec_c = sb("rec_c", [P, 16], FP32)
        Mt = sb("Mt", [H, MROWS, L], BF16)
        mx = sb("mx", [P, TT, H], FP32)

        X1s = sb("X1s", [P, 2, TC, E], FP32)
        xc = sb("xc", [P, 2, TC, E], BF16)
        nf = sb("nf", [P, TC, E], BF16)
        x2b = sb("x2b", [P, TC, E], BF16)
        nfT = sb("nfT", [P, CT, C], BF16)
        acc = sb("acc", [P, TC, E], FP32)
        combT = sb("combT", [NE, C], FP32)
        W1 = sb("W1", [P, 2, CT, 2 * FI], BF16)
        W2b = sb("W2b", [P, 2, CT * E], BF16)
        W2 = sb("W2", [P, 2, CT * E], FP32R)
        act_hi = sb("act_hi", [P, 2, CT, C], FP32R)
        act_lo = sb("act_lo", [P, 2, CT, C], FP32R)
        g_sb = sb("g_sb", [P, 2, C], FP32)
        l_sb = sb("l_sb", [P, 2, C], FP32)
        th_sb = sb("th_sb", [P, 2, C], FP32)
        act_sb = sb("act_sb", [P, 2, C], FP32)

        st1, st2 = sb("st1", [P, TC, 6], FP32), sb("st2", [P, TC, 6], FP32)
        mv1, mv2 = sb("mv1", [P, TC, 2], FP32), sb("mv2", [P, TC, 2], FP32)
        var1, rstd1, var2, rstd2, ss, ms, rrms, top1, top2, pickm, dtop, etop, w_1, w_2 = (
            sb(n, [P, TC], FP32) for n in ("var1", "rstd1", "var2", "rstd2", "ss", "ms", "rrms", "top1", "top2",
                                           "pickm", "dtop", "etop", "w_1", "w_2"))
        sqs = sb("sqs", [P, E], FP32)
        nsq = sb("nsq", [P, 2, 4], FP32)
        nsq2 = sb("nsq2", [P, 2], FP32)
        nsqa = sb("nsqa", [P, 2], FP32)
        bound = sb("bound", [P, 1], FP32)
        exact_flag = sb("exact_flag", [P, B], INT32)
        lgb = sb("lgb", [P, TC, NE], BF16)
        lgt, pick, oh1, oh2, lg2, comb, combh = (
            sb(n, [P, TC, NE], FP32) for n in ("lgt", "pick", "oh1", "oh2", "lg2", "comb", "combh"))

        S = ps("S", [P, 2, 2 * C], FP32)
        OP = ps("OP", [P, C], FP32)
        A = ps("A", [P, C], FP32)
        BB = ps("BB", [P, C], FP32)
        D = ps("D", [P, C], FP32)

        c_ld, c_late, c_set, c_set2, passed = (sem(n) for n in ("c_ld", "c_late", "c_set", "c_set2", "passed"))
        d_full = sem("d_full")
        x_ld, stat1, aggr1, var1_s, rstd1_s, xn_s, xnT_s = (
            sem(n) for n in ("x_ld", "stat1", "aggr1", "var1_s", "rstd1_s", "xn_s", "xnT_s"))
        qk_b, qk_sw, qk_cos, qk_sin, qk_rot, qk_p1, qk_sq, qk_r1, qk_p2, qk_p3 = (
            sem(n) for n in ("qk_b", "qk_sw", "qk_cos", "qk_sin", "qk_rot", "qk_p1", "qk_sq", "qk_r1", "qk_p2", "qk_p3"))
        scr_w = [sem("scr_w0"), sem("scr_w1")]
        nrm_red, nsq_s, nsqa_s, bound_s, flag_s = (sem(n) for n in ("nrm_red", "nsq_s", "nsqa_s", "bound_s", "flag_s"))
        vn_s, v_s = sem("vn_s"), sem("v_s")
        ex_ld = [sem("ex_ld0"), sem("ex_ld1")]
        ex_mm, ex_red, ex_t, m_set, m_w, m_zero = (sem(n) for n in ("ex_mm", "ex_red", "ex_t", "m_set", "m_w", "m_zero"))
        st_ld = [sem("st_ld0"), sem("st_ld1")]
        s_done, exp_done, av_done = sem("s_done"), sem("exp_done"), sem("av_done")
        o_ev, o_w, o_r, sum_r, rec_s, rec_w, rec_r, on_s = (
            sem(n) for n in ("o_ev", "o_w", "o_r", "sum_r", "rec_s", "rec_w", "rec_r", "on_s"))
        x1_ld, x1_b, x1_s, stat2, aggr2, var2_s, rstd2_s, xc_s, ss_s, ms_s, rrms_s, nf_s, nfT_s = (
            sem(n) for n in ("x1_ld", "x1_b", "x1_s", "stat2", "aggr2", "var2_s", "rstd2_s", "xc_s", "ss_s", "ms_s",
                             "rrms_s", "nf_s", "nfT_s"))
        gating, dtop_s, etop_s, comb_s, combT_s, acc_s = (
            sem(n) for n in ("gating", "dtop_s", "etop_s", "comb_s", "combT_s", "acc_s"))
        w1_ld, w2_ld = [sem("w1_ld0"), sem("w1_ld1")], [sem("w2_ld0"), sem("w2_ld1")]
        w2_s, m1_mm, g_s, l_s, th_s, t1_s, act_s, hi_s, lo_s, m2_mm, m2_ev = (
            sem(n) for n in ("w2_s", "m1_mm", "g_s", "l_s", "th_s", "t1_s", "act_s", "hi_s", "lo_s", "m2_mm", "m2_ev"))
        cb_s, fo_s, x2_s, out_w = sem("cb_s"), sem("fo_s"), sem("x2_s"), sem("out_w")

        N_LOADS, N_LATE = 6, 11
        N_CONST_SET2 = 5
        STACK = 16 * (2 * len(PRODUCTS) + 1)
        EX_STACK = 16 * 2 * len(PRODUCTS)
        GATES1, GATING = 13, 18
        PAIRS = 2 * STEPS

        x_v = x.rearrange("b (n t p) c -> (b n) p t c", p=P, t=TC)
        out_v = out.rearrange("b (n t p) c -> (b n) p t c", p=P, t=TC)

        def bank_of(filling):
            k, _, ahead = filling
            return (D, A, BB, OP)[k % HEAD_BANKS] if ahead else D

        def in_head(u):
            return not looped(u) and u < NCH

        def alone(u):
            return not looped(u) and u == B * NCH - 1

        def expert_banks(u, i):
            if alone(u):
                s_banks = [S[:, k // 2, C * (k % 2):C * (k % 2 + 1)] for k in range(4)]
                return (A[:, :], s_banks[0])[i % 2], (BB[:, :], s_banks[1])[i % 2], s_banks[2 + i % 2]
            return A[:, :], BB[:, :], D[:, :]

        def wait_apart(engine, *waits):
            for signal, value in waits:
                engine.wait_ge(signal, value)
                engine.sem_inc(passed, 1)

        FILLED0 = NCH * PREP_FILLS
        FILLED1 = FILLED0 + NCH * PREP_FILLS + POST_FILLS
        LOOP_FILLS = NCH * (PREP_FILLS + POST_FILLS)
        FILLED3 = FILLED1 + 2 * LOOP_FILLS
        FILLED4 = FILLED3 + NCH * POST_FILLS

        def run(engine, beside, stage, attend, start, turn):
            beside.at(0, 0, 0, False, False)
            for now in beside.head():
                stage(*now)
            start()
            turn(0)

            def body(b, prep, base):
                beside.at(base, b - 1, NCH - 1, True, looped(b) or b >= 1)
                for n in range(NCH):
                    w = NCH * b + n
                    for s in range(STEPS):
                        def aside(place):
                            for now in beside.stages(b, n, s, place, prep, looped(b) or w >= 1, looped(b) or w >= 2):
                                stage(*now)
                        attend(b, n, s, prep, aside)
                if prep:
                    turn(b + 1)

            body(0, True, FILLED0)
            with engine.Fori(1, B - 1) as b:
                body(b, True, FILLED1 + LOOP_FILLS * (b - 1))
            body(B - 1, False, FILLED3)
            beside.at(FILLED4, B - 1, NCH - 1, False, True)
            for step in range(FINAL + 1):
                for place in range(2):
                    attend(B, 0, step, False, None, place)
                    left = (B, 0, step, place, False, True, True) if step < STEPS else (B, 1, step - STEPS, place, False, False, True)
                    for now in beside.stages(*left):
                        stage(*now)

        block = ctx.enter_context(nc.Block())

        @block.sync
        def _(sp):
            loads = (
                (ident[:, :], ident_in), (wqk_sb[:, :, :], wqk.rearrange("(c p) n -> p c n", p=P)), (bqk_sb[:, :], bqk),
                (cos_sb[:, :], rope[0]), (sin_sb[:, :], rope[1]), (same_head_f[:, :], heads_in),
            )
            late = (
                (wv_sb[:, :, :], wv.rearrange("(c p) n -> p c n", p=P)), (bv_sb[:, :], bv[None, :].to_broadcast([P, E])),
                (wo_sb[:, :, :], wo.rearrange("(c p) n -> p c n", p=P)), (bo_sb[:, :], bo[None, :].to_broadcast([P, E])),
                (nw_sb[:, :], nw[None, :].to_broadcast([P, E])),
                (gate_sb[:, :, :], gate.rearrange("(c p) n -> p c n", p=P)),
                (gate_b_sb[:, :], gate_b[None, :].to_broadcast([P, NE])),
                (b1_sb[:, :, :, :], b1), (b2_sb[:, :], b2), (rank[:, :], rank_in[None, :].to_broadcast([P, NE])),
                (Ks[SROWS:SROWS + MROWS, :, :, :].rearrange("p s j t -> p (s j t)"), ones_in),
            )
            assert len(loads) == N_LOADS and len(late) == N_LATE

            def stack(b, n, g, signal, shifts):
                row, ch = 0, slice(HG * HD * g, HG * HD * (g + 1))
                for part, blocks in PRODUCTS:
                    rows = slice(row, row + HD * blocks)
                    sp.dma_start(Qs[rows, g % 2, :, :].rearrange("p j t -> p (j t)"),
                                 q_scr[b, n, part, ch, :].rearrange("(d j) t -> d (j t)", j=HG)[None].to_broadcast([blocks, HD, HG * C])
                                 ).then_inc(signal, 16)
                    sp.dma_start(Ks[rows, g % 2, :, :].rearrange("p j t -> p (j t)"),
                                 k_scr[b, 0:blocks, ch, :].rearrange("a (d j) t -> a d (j t)", j=HG)).then_inc(signal, 16)
                    row += HD * blocks
                if shifts:
                    sp.dma_start(Qs[SROWS:SROWS + MROWS, g % 2, :, :],
                                 m_scr[b, :, HG * g:HG * (g + 1), C * n:C * (n + 1)]).then_inc(signal, 16)

            def flag_of(b):
                return sp.value_load(exact_flag[0:1, bass.ds(b, 1)], min_val=0, max_val=1)

            def stage(st, a, bb, n, filling):
                k, bank = filling[0], bank_of(filling)
                u = NCH * bb + n
                if st == "weights":
                    sp.wait_ge(c_set2, N_CONST_SET2)
                    for i in range(B):
                        sp.dma_start(m_scr[i].rearrange("r h t -> h r t"), Mt[:, :, :]).then_inc(m_zero, 16)
                elif st == "x_in":
                    if looped(u) or u >= 1:
                        sp.wait_ge(xn_s, TC * u)
                    sp.dma_start(X[:, :, :], x_v[bass.ds(u, 1)].rearrange("o p t c -> (o p) t c")).then_inc(x_ld, 16)
                elif st == "part3":
                    sp.wait_ge(qk_p3, 4 * u + a + 1)
                    ch = slice(P * (a % 2), P * (a % 2 + 1))
                    to = q_scr[bb, n, :, ch, :] if a < 2 else k_scr[bb, :, ch, C * n:C * (n + 1)]
                    sp.dma_start(to.rearrange("a p t -> p a t"), parts[:, a % 2, :, :]).then_inc(scr_w[a % 2], 16)
                elif st == "x1_in":
                    if looped(bb) or bb:
                        sp.wait_ge(acc_s, 2 * u)
                    sp.dma_start(X1s[:, n, :, :], x_v[bass.ds(u, 1)].rearrange("o p t c -> (o p) t c")).then_inc(x1_ld, 16)
                elif st == "final":
                    sp.wait_ge(x2_s, 2 * (u + 1))
                    sp.dma_start(out_v[bass.ds(u, 1)].rearrange("o p t c -> (o p) t c"), acc[:, :, :]).then_inc(out_w, 16)

            def output_way(b, n, g, kt, place):
                u = NCH * b + n
                G = NG * u + g
                if (kt, place) == (0, 1):
                    sp.wait_ge(o_ev, G + 1)
                    sp.dma_start(o_scr[bass.ds(u, 1), g].rearrange("o p t -> (o p) t"), O[:, g % 2, :]).then_inc(o_w, 16)
                if (kt, place) == (1, 1):
                    wait_apart(sp, (o_w, 16 * (G + 1)))
                    for j in range(HG):
                        r = 32 * j + HD
                        sp.dma_start(sums_c[32 * j:32 * (j + 1), :],
                                     o_scr[bass.ds(u, 1), g, r:r + 1, :].rearrange("o h (j t) -> (o h j) t", t=16)).then_inc(sum_r, 16)
                    if g == 0 and (looped(u) or u >= 1):
                        wait_apart(sp, (x1_s, 2 * u))
                    for j in range(HG):
                        r = 64 * (g % 2) + HD * j
                        sp.dma_start(Op[r:r + HD, g // 2, :],
                                     o_scr[bass.ds(u, 1), g, 32 * j:32 * j + HD, :].rearrange("o p t -> (o p) t")).then_inc(o_r, 16)
                if (kt, place) == (3, 0):
                    sp.wait_ge(rec_s, G + 1)
                    sp.dma_start(rec_scr[bass.ds(u, 1), g].rearrange("o h (j t) -> (o h j) t", t=16), rec_c[:, :]).then_inc(rec_w, 16)
                if (kt, place) == (4, 0):
                    wait_apart(sp, (rec_w, 16 * (G + 1)))
                    if g % 2 == 0 and (looped(u) or u >= 1 or g):
                        wait_apart(sp, (on_s, 2 * u + g // 2))
                    for j in range(HG):
                        r = 64 * (g % 2) + HD * j
                        sp.dma_start(rec_b[r:r + HD, :],
                                     rec_scr[bass.ds(u, 1), g, j:j + 1, :].rearrange("o h t -> (o h) t").to_broadcast([HD, C])
                                     ).then_inc(rec_r, 16)

            def attend(b, n, s, prep, aside, place=None):
                g, kt = divmod(s, KT)
                for pl in range(2) if place is None else (place,):
                    if not (isinstance(b, int) and b == 0 and n == 0 and g == 0) and s < STEPS:
                        if g:
                            output_way(b, n, g - 1, kt, pl) if b is not B or g == 0 else None
                        elif n:
                            output_way(b, 0, NG - 1, kt, pl)
                        else:
                            output_way(b - 1, NCH - 1, NG - 1, kt, pl)
                    if aside is not None:
                        aside(pl)
                if aside is not None and kt == KT - 1:
                    done = 2 * KT * (NG * (NCH * b + n) + g + 1)
                    if g < 2 or n == 0:
                        sp.wait_ge(s_done, done)
                        stack(b, n if g < 2 else n + 1, (g + 2) % NG, st_ld[g % 2], True)
                    elif prep:
                        wait_apart(sp, (s_done, done), (scr_w[0], 64 * (b + 2)), (scr_w[1], 64 * (b + 2)), (flag_s, b + 2))
                        with sp.If(flag_of(b + 1) < 1):
                            stack(b + 1, 0, g - 2, st_ld[g % 2], True)

            def turn(b):
                wait_apart(sp, (scr_w[0], 64 * (b + 1)), (scr_w[1], 64 * (b + 1)), (flag_s, b + 1), (m_zero, 16 * B))
                with sp.If(flag_of(b) > 0):
                    if not (isinstance(b, int) and b == 0):
                        wait_apart(sp, (s_done, NCH * PAIRS * b))
                    for n in range(NCH):
                        for g in range(NG):
                            if g >= 2 or n:
                                wait_apart(sp, (ex_mm, 128 * b + 16 * (NG * n + g - 1)))
                            stack(b, n, g, ex_ld[g % 2], False)
                    wait_apart(sp, (m_set, 2 * (b + 1)))
                    sp.dma_start(m_scr[b].rearrange("r h t -> h r t"), Mt[:, :, :]).then_inc(m_w, 16)
                    wait_apart(sp, (m_w, 16 * (b + 1)))
                    stack(b, 0, 0, st_ld[0], True)
                    stack(b, 0, 1, st_ld[1], True)
                with sp.If(flag_of(b) < 1):
                    for slot in range(2):
                        sp.sem_inc(ex_ld[slot], 4 * EX_STACK)
                    sp.sem_inc(m_w, 16)
                    if isinstance(b, int) and b == 0:
                        stack(b, 0, 0, st_ld[0], True)
                        stack(b, 0, 1, st_ld[1], True)

            stage("x_in", 0, 0, 0, (0, None, True))
            for dst, src in loads:
                sp.dma_start(dst, src).then_inc(c_ld, 16)
            for dst, src in late:
                sp.dma_start(dst, src).then_inc(c_late, 16)
            run(sp, Beside(), stage, attend, lambda: None, turn)
            sp.wait_ge(out_w, 16 * B * NCH)

        @block.tensor
        def _(pe):
            mm = nc.tensor.matmul

            def read_of(st, a, u):
                return {"xT": (xnT_s, 2 * u + a + 1), "qk": (qk_b, 4 * u + a + 1), "length": (nrm_red, 4 * u + a + 1),
                        "v": (vn_s, 2 * u + a + 1), "wo": (x1_s, 2 * u + a + 1), "nfT": (nfT_s, u + 1),
                        "down": (m2_ev, 2 * (NF * u + a + 1)), "logits": (gating, GATING * u + 1), "combT": (combT_s, u + 1), "b2": (acc_s, 2 * u + a + 1)}[st]

            def stage(st, a, bb, n, filling):
                k, bank = filling[0], bank_of(filling)
                u = NCH * bb + n
                if st in FILLS and filling[1]:
                    pe.wait_ge(*read_of(*filling[1]))
                if st == "weights":
                    pe.wait_ge(c_late, 16 * N_LATE)
                elif st == "early":
                    pe.wait_ge(c_set, 4)
                elif st == "xT":
                    pe.wait_ge(xn_s, TC * (u + 1))
                    for t in range(TC):
                        last = nc.tensor.transpose(bank[:, P * t:P * (t + 1)], xn[:, t, P * a:P * (a + 1)], ident[:, :])
                    last.then_inc(d_full, 1)
                elif st == "qk":
                    pe.wait_ge(xnT_s, 2 * (u + 1))
                    for c in range(CT):
                        last = mm(bank[:, :], wqk_sb[:, c, P * a:P * (a + 1)], xnT[:, c, :], start=c == 0, stop=c == CT - 1)
                    last.then_inc(d_full, 1)
                elif st == "length":
                    pe.wait_ge(qk_sq, 4 * u + a + 1)
                    mm(bank[:, :], same_head[:, :], sq[:, :], start=True, stop=True).then_inc(d_full, 1)
                elif st == "v":
                    for t in range(2):
                        for c in range(CT):
                            last = mm(bank[:, E * t:E * (t + 1)], xnT[:, c, P * (2 * a + t):P * (2 * a + t + 1)], wv_sb[:, c, :],
                                      start=c == 0, stop=c == CT - 1)
                    last.then_inc(d_full, 1)
                elif st == "wo":
                    pe.wait_ge(on_s, 2 * (u + 1))
                    for t in range(2):
                        tok = P * (2 * a + t)
                        for c in range(CT):
                            last = mm(bank[:, E * t:E * (t + 1)], Op[:, c, tok:tok + P], wo_sb[:, c, :],
                                      start=c == 0, stop=c == CT - 1)
                    last.then_inc(d_full, 1)
                elif st == "nfT":
                    pe.wait_ge(nf_s, TC * (u + 1))
                    for c in range(CT):
                        for t in range(TC):
                            last = nc.tensor.transpose(bank[:, :].bitcast(BF16)[:, C * c + P * t:C * c + P * (t + 1)],
                                                       nf[:, t, P * c:P * (c + 1)], identb[:, :])
                    last.then_inc(d_full, 1)
                elif st == "logits":
                    pe.wait_ge(nfT_s, u + 1)
                    for t in range(TC):
                        for c in range(CT):
                            last = mm(bank[:, NE * t:NE * (t + 1)], nfT[:, c, P * t:P * (t + 1)], gate_sb[:, c, :],
                                      start=c == 0, stop=c == CT - 1)
                    last.then_inc(d_full, 1)
                elif st == "combT":
                    pe.wait_ge(comb_s, 3 * (u + 1))
                    for t in range(TC):
                        last = nc.tensor.transpose(bank[0:NE, P * t:P * (t + 1)], comb[:, t, :], ident[:, :])
                    last.then_inc(d_full, 1)
                elif st == "b2":
                    pe.wait_ge(combT_s, u + 1)
                    for t in range(2):
                        tok = P * (2 * a + t)
                        last = mm(bank[:, E * t:E * (t + 1)], combT[:, tok:tok + P], b2f[:, :], start=True, stop=True)
                    last.then_inc(d_full, 1)
                elif st == "up":
                    expert_up(a, u)
                elif st == "down":
                    if not alone(u):
                        pe.wait_ge(*read_of(*filling[1]))
                    expert_down(a, u)

            def expert_up(f, u):
                e, it = divmod(f, 2)
                if it == 0:
                    pe.wait_ge(w1_ld[e % 2], 16 * (4 * u + e // 2 + 1))
                if f == 0:
                    pe.wait_ge(nfT_s, u + 1)
                if alone(u):
                    if f == 0:
                        pe.wait_ge(exp_done, PAIRS * B * NCH)
                    if f >= 2:
                        pe.wait_ge(g_s, NF * u + f - 1)
                elif f:
                    pe.wait_ge(g_s, NF * u + f)
                gate, linear, _ = expert_banks(u, f)
                for gl, bank in ((0, gate), (1, linear)):
                    if gl and alone(u) and f >= 2:
                        pe.wait_ge(l_s, NF * u + f - 1)
                    elif gl and not alone(u) and f:
                        pe.wait_ge(l_s, NF * u + f)
                    for c in range(CT):
                        last = mm(bank, W1[:, e % 2, c, FI * gl + P * it:FI * gl + P * (it + 1)], nfT[:, c, :],
                                  start=c == 0, stop=c == CT - 1)
                    last.then_inc(m1_mm, 1)

            def expert_down(m, u):
                e, hh = divmod(m, 2)
                if hh == 0:
                    pe.wait_ge(lo_s, NF * u + m + 2)
                    pe.wait_ge(w2_s, NE * u + e + 1)
                if alone(u) and m >= 2:
                    pe.wait_ge(m2_ev, 2 * (NF * u + m - 1))
                bank = expert_banks(u, m)[2]
                for q in range(2):
                    tok = P * (2 * hh + q)
                    for k in range(4):
                        it, part = k // 2, (act_hi, act_lo)[k % 2]
                        last = mm(bank[:, E * q:E * (q + 1)], part[:, e % 2, it, tok:tok + P], W2[:, e % 2, E * it:E * (it + 1)],
                                  start=k == 0, stop=k == 3)
                last.then_inc(m2_mm, 1)

            def scores(b, n, s, j2):
                g, kt = divmod(s, KT)
                u = NCH * b + n
                if j2 == 0 and kt == 0:
                    pe.wait_ge(st_ld[g % 2], STACK * (2 * u + g // 2 + 1))
                if s or n or looped(b) or b:
                    pe.wait_ge(exp_done, PAIRS * u + 2 * s + j2 - 1)
                for i in range(2):
                    j = 2 * j2 + i
                    last = mm(S[:, j2, C * i:C * (i + 1)], Ks[0:SROWS + MROWS, g % 2, j, P * kt:P * (kt + 1)],
                              Qs[0:SROWS + MROWS, g % 2, j, :], start=True, stop=True)
                last.then_inc(s_done, 1)

            def values(b, n, s):
                g, kt = divmod(s, KT)
                u = NCH * b + n
                pe.wait_ge(exp_done, PAIRS * u + 2 * (s + 1))
                if n == 0 and g == 0:
                    pe.wait_ge(v_s, KT * b + kt + 1)
                if kt == 0 and (g or n or looped(b) or b):
                    pe.wait_ge(o_ev, NG * u + g)
                for j in range(HG):
                    last = mm(OP[32 * j:32 * j + VW, :], V[:, kt, HG * g + j, :], probs[:, s % 2, C * j:C * (j + 1)],
                              start=kt == 0, stop=kt == KT - 1)
                last.then_inc(av_done, 1)

            def attend(b, n, s, prep, aside, place=None):
                if aside is None:
                    return
                after = (b, n, s + 1) if s + 1 < STEPS else (b, n + 1, 0) if n + 1 < NCH else None
                if after:
                    scores(*after, 0)
                aside(0)
                if after:
                    scores(*after, 1)
                values(b, n, s)
                aside(1)

            def turn(b):
                wait_apart(pe, (flag_s, b + 1))
                flag = pe.value_load(exact_flag[0:1, bass.ds(b, 1)], min_val=0, max_val=1)
                with pe.If(flag > 0):
                    if not (isinstance(b, int) and b == 0):
                        wait_apart(pe, (exp_done, NCH * PAIRS * b))
                    for n in range(NCH):
                        for g in range(NG):
                            wait_apart(pe, (ex_ld[g % 2], EX_STACK * (4 * b + 2 * n + g // 2 + 1)))
                            for j in range(HG):
                                for t in range(TC):
                                    i = 16 * (NG * n + g) + TC * j + t
                                    if i >= 2:
                                        wait_apart(pe, (ex_red, 128 * b + i - 1))
                                    for hf in range(2):
                                        last = mm(S[:, i % 2, C * hf:C * (hf + 1)], Qs[0:SROWS, g % 2, j, P * t:P * (t + 1)],
                                                  Ks[0:SROWS, g % 2, j, C * hf:C * (hf + 1)], start=True, stop=True)
                                    last.then_inc(ex_mm, 1)
                    wait_apart(pe, (ex_red, 128 * (b + 1)))
                    for t in range(TT):
                        last = nc.tensor.transpose(S[0:H, 0, P * t:P * (t + 1)], mx[:, t, :], ident[:, :])
                    last.then_inc(ex_t, 1)
                    wait_apart(pe, (m_set, 2 * (b + 1)))
                with pe.If(flag < 1):
                    pe.sem_inc(ex_mm, 128)
                    pe.sem_inc(ex_t, 1)
                scores(b, 0, 0, 0)
                scores(b, 0, 0, 1)

            pe.wait_ge(c_ld, 16 * N_LOADS)
            run(pe, Beside(), stage, attend, lambda: pe.wait_ge(c_set2, N_CONST_SET2), turn)

        @block.scalar
        def _(act):
            def stage(st, a, bb, n, filling):
                k, bank = filling[0], bank_of(filling)
                u = NCH * bb + n
                if st == "xT" and a == 0:
                    act.wait_ge(d_full, k + 1)
                    nc.scalar.copy(xnT[:, 0, :], bank[:, :]).then_inc(xnT_s, 1)
                elif st == "qk":
                    act.wait_ge(d_full, k + 1)
                    if looped(u) or u or a >= 2:
                        act.wait_ge(qk_sw, 4 * u + a - 1)
                        act.wait_ge(qk_cos, 4 * u + a - 1)
                    nc.scalar.activation(qb[:, a % 2, :], bank[:, :], ACT.Identity, bias=bqk_sb[:, a:a + 1]).then_inc(qk_b, 1)
                elif st == "part1":
                    act.wait_ge(qk_rot, 4 * u + a + 1)
                    if looped(u) or u or a >= 2:
                        act.wait_ge(scr_w[a % 2], 32 * u + 16 * (a // 2))
                    nc.scalar.copy(parts[:, a % 2, 0, :], rot[:, a % 2, :]).then_inc(qk_p1, 1)
                    if looped(u) or u or a:
                        act.wait_ge(nrm_red, 4 * u + a)
                    nc.scalar.activation(sq[:, :], rot[:, a % 2, :], ACT.Square).then_inc(qk_sq, 1)
                elif st == "part2":
                    act.wait_ge(qk_r1, 4 * u + a + 1)
                    nc.scalar.copy(parts[:, a % 2, 1, :], sw[:, a % 2, :]).then_inc(qk_p2, 1)
                elif st == "ss":
                    for t in range(TC):
                        act.wait_ge(xc_s, TC * u + t + 1)
                        if t:
                            act.wait_ge(ss_s, TC * u + t)
                        nc.scalar.activation(sqs[:, :], xc[:, n, t, :], ACT.Square, accum_out=ss[:, t:t + 1]).then_inc(ss_s, 1)
                elif st == "nfT":
                    act.wait_ge(d_full, k + 1)
                    nc.scalar.copy(nfT[:, :, :].rearrange("p c t -> p (c t)"), bank[:, :].bitcast(BF16)).then_inc(nfT_s, 1)
                elif st == "etop":
                    act.wait_ge(dtop_s, u + 1)
                    nc.scalar.activation(etop[:, :], dtop[:, :], ACT.Exp).then_inc(etop_s, 1)
                elif st == "hidden" and alone(u):
                    upper_half(a, u)
                elif st == "tanh":
                    act.wait_ge(g_s, NF * u + a + 1)
                    if looped(u) or u or a >= 2:
                        act.wait_ge(act_s, NF * u + a - 1)
                    nc.scalar.activation(th_sb[:, a % 2, :], g_sb[:, a % 2, :], ACT.Tanh, scale=ALPHA / 2).then_inc(th_s, 1)
                    e, it = divmod(a, 2)
                    if it == 1 and (looped(u) or e + 2 < NE or u + 1 < B * NCH):
                        wait_apart(act, (m1_mm, 4 * NE * u + 4 * (e + 1)), (w2_s, NE * u + e + 1))
                        load_expert((e + 2) % NE)

            def upper_half(a, u):
                e, it = divmod(a, 2)
                act.wait_ge(act_s, NF * u + a + 1)
                if e >= 2:
                    act.wait_ge(m2_mm, NF * u + 2 * (e - 1))
                nc.scalar.copy(act_hi[:, e % 2, it, :], act_sb[:, a % 2, :]).then_inc(hi_s, 1)

            def load_expert(e):
                act.dma_start(W1[:, e % 2, :, :], w1[e]).then_inc(w1_ld[e % 2], 16)
                act.dma_start(W2b[:, e % 2, :], w2[e]).then_inc(w2_ld[e % 2], 16)

            def exps(b, n, s, j2):
                u = NCH * b + n
                act.wait_ge(s_done, PAIRS * u + 2 * s + j2 + 1)
                if j2 == 0 and (s >= 2 or n or looped(b) or b):
                    act.wait_ge(av_done, STEPS * u + s - 1)
                nc.scalar.activation(probs[:, s % 2, 2 * C * j2:2 * C * (j2 + 1)], S[:, j2, :], ACT.Exp,
                                     scale=SCALE).then_inc(exp_done, 1)

            def take_output(b, n, g):
                G = NG * (NCH * b + n) + g - 1
                act.wait_ge(av_done, KT * (G + 1))
                if looped(G) or G >= 2:
                    act.wait_ge(o_w, 16 * (G - 1))
                nc.scalar.copy(O[:, (g - 1) % 2, :], OP[:, :]).then_inc(o_ev, 1)

            def attend(b, n, s, prep, aside, place=None):
                g, kt = divmod(s, KT)
                if kt == 0 and (g or n or looped(b) or b) and (aside is not None or (g, place) == (0, 0)):
                    take_output(b, n, g)
                if aside is None:
                    return
                if n == 0 and s == 0:
                    exps(b, 0, 0, 0)
                    exps(b, 0, 0, 1)
                after = (b, n, s + 1) if s + 1 < STEPS else (b, n + 1, 0) if n + 1 < NCH else None
                if after:
                    exps(*after, 0)
                aside(0)
                if after:
                    exps(*after, 1)
                aside(1)

            act.wait_ge(c_ld, 16 * N_LOADS)
            for slot in range(2):
                load_expert(slot)
            run(act, Beside(), stage, attend, lambda: None, lambda b: None)

        @block.gpsimd
        def _(pool):
            tt = nc.gpsimd.tensor_tensor

            def stage(st, a, bb, n, filling):
                k, bank = filling[0], bank_of(filling)
                u = NCH * bb + n
                if st == "early":
                    pool.wait_ge(c_ld, 16 * N_LOADS)
                elif st == "rstd1":
                    pool.wait_ge(var1_s, u + 1)
                    tt(rstd1[:, :], var1[:, :], half_pow[:, :], ALU.pow).then_inc(rstd1_s, 1)
                elif st == "rope":
                    cols, q = slice(C * n, C * (n + 1)), a % 2
                    if not in_head(u):
                        pool.wait_ge(qk_b, 4 * u + a + 1)
                        pool.wait_ge(qk_r1, 4 * u + a - 1)
                        pool.wait_ge(qk_sq, 4 * u + a - 1)
                        tt(rot[:, q, :], qb[:, q, :], cos_sb[:, cols], ALU.mult).then_inc(qk_cos, 1)
                    pool.wait_ge(qk_sw, 4 * u + a + 1)
                    tt(sw[:, q, :], sw[:, q, :], sin_sb[:, cols], ALU.mult).then_inc(qk_sin, 1)
                    if not in_head(u):
                        pool.wait_ge(qk_cos, 4 * u + a + 1)
                        pool.wait_ge(qk_sin, 4 * u + a + 1)
                        tt(rot[:, q, :], rot[:, q, :], sw[:, q, :], ALU.add).then_inc(qk_rot, 1)
                elif st == "length":
                    pool.wait_ge(qk_p1, 4 * u + a + 1)
                    tt(sw[:, a % 2, :], rot[:, a % 2, :], parts[:, a % 2, 0, :], ALU.subtract).then_inc(qk_r1, 1)
                elif st == "guard" and n == NCH - 1:
                    wait_apart(pool, (nsq_s, bb + 1))
                    nc.gpsimd.partition_all_reduce(nsqa[:, :], nsq2[:, :], P, bass.bass_isa.ReduceOp.max).then_inc(nsqa_s, 1)
                elif st == "x1_b":
                    wait_apart(pool, (x1_ld, 16 * (u + 1)))
                    tt(X1s[:, n, :, :], X1s[:, n, :, :], bo_sb[:, None, :].to_broadcast([P, TC, E]), ALU.add).then_inc(x1_b, 1)
                elif st == "rstd2":
                    pool.wait_ge(var2_s, u + 1)
                    tt(rstd2[:, :], var2[:, :], half_pow[:, :], ALU.pow).then_inc(rstd2_s, 1)
                elif st == "rrms":
                    pool.wait_ge(ms_s, u + 1)
                    tt(rrms[:, :], ms[:, :], half_pow[:, :], ALU.pow).then_inc(rrms_s, 1)
                elif st == "w2":
                    e, it = divmod(a, 2)
                    if it == 0:
                        wait_apart(pool, (w2_ld[e % 2], 16 * (4 * u + e // 2 + 1)))
                        if looped(u) or u or e >= 2:
                            wait_apart(pool, (m2_mm, NF * u + 2 * (e - 1)))
                        nc.gpsimd.tensor_scalar(W2[:, e % 2, :], W2b[:, e % 2, :], 1.0, 1.0, ALU.mult, ALU.mult).then_inc(w2_s, 1)
                elif st == "lo":
                    e, it = divmod(a, 2)
                    if looped(u) or u or e >= 2:
                        pool.wait_ge(m2_mm, NF * u + 2 * (e - 1))
                    pool.wait_ge(hi_s, NF * u + a + 1)
                    tt(act_lo[:, e % 2, it, :], act_sb[:, a % 2, :], act_hi[:, e % 2, it, :].bitcast(FP32),
                       ALU.subtract).then_inc(lo_s, 1)

            def attend(b, n, s, prep, aside, place=None):
                g, kt = divmod(s, KT)
                if kt == 5 and place in (None, 0) and g % 2 == 0 and s < STEPS \
                        and not (isinstance(b, int) and b == 0 and n == 0 and g == 0):
                    u, c = (NCH * b + n, 0) if g else (NCH * b + n - 1, 1)
                    if b is not B or g == 0:
                        pool.wait_ge(rec_r, 64 * (NG * u + 2 * (c + 1)))
                        pool.wait_ge(o_r, 64 * (NG * u + 2 * (c + 1)))
                        tt(Op[:, c, :], Op[:, c, :], rec_b[:, :], ALU.mult).then_inc(on_s, 1)
                if aside is not None:
                    aside(0)
                    aside(1)

            pool.wait_ge(c_set, 1)
            run(pool, Beside(), stage, attend, lambda: pool.wait_ge(c_late, 16 * N_LATE), lambda b: None)

        @block.vector
        def _(dve):
            v = nc.vector

            def norm_stats(src, st, mv, var, stat_s, aggr_s, var_s, u):
                for t in range(TC):
                    v.bn_stats(st[:, t, :], src[:, t, :]).then_inc(stat_s, 1)
                for t in range(TC):
                    wait_apart(dve, (stat_s, TC * u + t + 1))
                    v.bn_aggr(mv[:, t, :], st[:, t, :]).then_inc(aggr_s, 1)
                dve.wait_ge(aggr_s, TC * (u + 1))
                v.tensor_scalar(var[:, :], mv[:, :, 1], EPS, None, ALU.add).then_inc(var_s, 1)

            def stage(st, a, bb, n, filling):
                k, bank = filling[0], bank_of(filling)
                u = NCH * bb + n
                if st == "early":
                    v.memset(V[:, :, :, HD:VW], 1.0).then_inc(c_set, 1)
                    dve.wait_ge(c_ld, 16 * N_LOADS)
                    v.tensor_copy(same_head[:, :], same_head_f[:, :]).then_inc(c_set, 1)
                elif st == "weights":
                    dve.wait_ge(c_late, 16 * N_LATE)
                    v.memset(Mt[:, :, :], 0.0).then_inc(c_set2, 1)
                    v.tensor_copy(identb[:, :], ident[:, :]).then_inc(c_set2, 1)
                    v.tensor_copy(b1f[:, :, 0, :], b1_sb[:, :, 0, :]).then_inc(c_set2, 1)
                    v.tensor_scalar(b1f[:, :, 1, :], b1_sb[:, :, 1, :], 1.0, None, ALU.add).then_inc(c_set2, 1)
                    v.tensor_copy(b2f[:, :], b2_sb[:, :]).then_inc(c_set2, 1)
                    dve.wait_ge(c_set2, N_CONST_SET2)
                elif st == "stats1":
                    dve.wait_ge(x_ld, 16 * (u + 1))
                    norm_stats(X, st1, mv1, var1, stat1, aggr1, var1_s, u)
                elif st == "xn":
                    dve.wait_ge(rstd1_s, u + 1)
                    for t in range(TC):
                        v.tensor_scalar(xn[:, t, :], X[:, t, :], mv1[:, t, 0:1], rstd1[:, t:t + 1],
                                        ALU.subtract, ALU.mult).then_inc(xn_s, 1)
                elif st == "xT" and a == 1:
                    dve.wait_ge(d_full, k + 1)
                    v.tensor_copy(xnT[:, 1, :], bank[:, :]).then_inc(xnT_s, 1)
                elif st == "rope":
                    wait_apart(dve, (qk_b, 4 * u + a + 1), *([(qk_p3, 4 * u + a - 1)] if looped(u) or u or a >= 2 else []))
                    v.stream_shuffle(sw[:, a % 2, :], qb[:, a % 2, :], [r ^ HG for r in range(32)]).then_inc(qk_sw, 1)
                    if in_head(u):
                        dve.wait_ge(qk_b, 4 * u + a + 1)
                        if u or a >= 2:
                            dve.wait_ge(qk_r1, 4 * u + a - 1)
                            dve.wait_ge(qk_sq, 4 * u + a - 1)
                        v.tensor_tensor(rot[:, a % 2, :], qb[:, a % 2, :], cos_sb[:, C * n:C * (n + 1)], ALU.mult).then_inc(qk_cos, 1)
                elif st == "sum":
                    dve.wait_ge(qk_cos, 4 * u + a + 1)
                    dve.wait_ge(qk_sin, 4 * u + a + 1)
                    v.tensor_tensor(rot[:, a % 2, :], rot[:, a % 2, :], sw[:, a % 2, :], ALU.add).then_inc(qk_rot, 1)
                elif st == "part3":
                    dve.wait_ge(qk_p2, 4 * u + a + 1)
                    v.tensor_tensor(parts[:, a % 2, 2, :], sw[:, a % 2, :], parts[:, a % 2, 1, :], ALU.subtract).then_inc(qk_p3, 1)
                elif st == "length":
                    t, hf = divmod(a, 2)
                    dve.wait_ge(d_full, k + 1)
                    v.reduce_max(nsq[:, t, 2 * hf + n:2 * hf + n + 1], bank[:, :], AX_X).then_inc(nrm_red, 1)
                elif st == "guard" and n == NCH - 1:
                    dve.wait_ge(nrm_red, 4 * (u + 1))
                    v.reduce_max(nsq2[:, :], nsq[:, :, :], AX_X).then_inc(nsq_s, 1)
                elif st == "flag" and n == NCH - 1:
                    dve.wait_ge(nsqa_s, bb + 1)
                    v.tensor_tensor(bound[:, :], nsqa[:, 0:1], nsqa[:, 1:2], ALU.mult).then_inc(bound_s, 1)
                    dve.wait_ge(bound_s, bb + 1)
                    v.tensor_scalar(exact_flag[:, bass.ds(bb, 1)], bound[:, :],
                                    (safe_score / SCALE) ** 2 / 1.05 if safe_score > 0 else -1.0, None, ALU.is_gt).then_inc(flag_s, 1)
                elif st == "v":
                    if n == 0 and a == 0 and (looped(bb) or bb):
                        dve.wait_ge(v_s, KT * bb)
                    dve.wait_ge(d_full, k + 1)
                    t = TC * n + 2 * a
                    v.tensor_tensor(Vn[:, t:t + 2, :, :], bank[:, :].rearrange("p (t h d) -> p t h d", t=2, h=H),
                                    bv_sb[:, :].rearrange("p (h d) -> p h d", h=H)[:, None, :, :].to_broadcast([P, 2, H, HD]),
                                    ALU.add).then_inc(vn_s, 1)
                elif st == "wo":
                    dve.wait_ge(x1_b, u + 1)
                    dve.wait_ge(d_full, k + 1)
                    xh = X1s[:, n, 2 * a:2 * a + 2, :].rearrange("p t c -> p (t c)")
                    v.tensor_tensor(xh, bank[:, :], xh, ALU.add).then_inc(x1_s, 1)
                elif st == "stats2":
                    dve.wait_ge(x1_s, 2 * (u + 1))
                    norm_stats(X1s[:, n], st2, mv2, var2, stat2, aggr2, var2_s, u)
                elif st == "xc":
                    dve.wait_ge(rstd2_s, u + 1)
                    for t in range(TC):
                        v.tensor_scalar(xc[:, n, t, :], X1s[:, n, t, :], mv2[:, t, 0:1], rstd2[:, t:t + 1],
                                        ALU.subtract, ALU.mult).then_inc(xc_s, 1)
                elif st == "ms":
                    dve.wait_ge(ss_s, TC * (u + 1))
                    v.tensor_scalar(ms[:, :], ss[:, :], 1.0 / E, EPS, ALU.mult, ALU.add).then_inc(ms_s, 1)
                elif st == "nf":
                    dve.wait_ge(rrms_s, u + 1)
                    for t in range(TC):
                        v.scalar_tensor_tensor(nf[:, t, :], xc[:, n, t, :], rrms[:, t:t + 1], nw_sb[:, :],
                                               ALU.mult, ALU.mult).then_inc(nf_s, 1)
                elif st == "logits":
                    dve.wait_ge(d_full, k + 1)
                    v.tensor_tensor(lgb[:, :, :], bank[:, 0:TC * NE].rearrange("p (t e) -> p t e", e=NE),
                                    gate_b_sb[:, None, :].to_broadcast([P, TC, NE]), ALU.add).then_inc(gating, 1)
                elif st == "gates1":
                    gates1(u)
                elif st == "gates2":
                    gates2(u)
                elif st == "combT":
                    dve.wait_ge(d_full, k + 1)
                    v.tensor_copy(combT[:, :], bank[0:NE, :]).then_inc(combT_s, 1)
                elif st == "b2":
                    dve.wait_ge(d_full, k + 1)
                    if looped(u) or u:
                        dve.wait_ge(out_w, 16 * u)
                    v.tensor_copy(acc[:, 2 * a:2 * a + 2, :].rearrange("p t c -> p (t c)"), bank[:, :]).then_inc(acc_s, 1)
                elif st in ("up", "hidden", "down"):
                    expert(st, a, u)
                elif st == "final":
                    final(u, n)

            def chain(u, k):
                done = [k]

                def link(ins):
                    done[0] += 1
                    ins.then_inc(gating, 1)
                    dve.wait_ge(gating, GATING * u + done[0])
                    return done[0]
                return link

            def over_experts(x):
                return x[:, :, None].to_broadcast([P, TC, NE])

            def gates1(u):
                link = chain(u, 1)

                def first_of(onehot, logits, top):
                    link(v.reduce_max(top[:, :], logits, AX_X))
                    link(v.tensor_tensor(pick[:, :, :], logits, over_experts(top), ALU.is_equal))
                    link(v.tensor_tensor(pick[:, :, :], pick[:, :, :], rank[:, None, :].to_broadcast([P, TC, NE]), ALU.mult))
                    link(v.reduce_max(pickm[:, :], pick[:, :, :], AX_X))
                    return link(v.tensor_tensor(onehot[:, :, :], pick[:, :, :], over_experts(pickm), ALU.is_equal))

                dve.wait_ge(gating, GATING * u + 1)
                link(v.tensor_copy(lgt[:, :, :], lgb[:, :, :]))
                first_of(oh1, lgt[:, :, :], top1)
                link(v.scalar_tensor_tensor(lg2[:, :, :], oh1[:, :, :], -3.0e38, lgt[:, :, :], ALU.mult, ALU.add))
                assert first_of(oh2, lg2[:, :, :], top2) == GATES1
                v.tensor_tensor(dtop[:, :], top2[:, :], top1[:, :], ALU.subtract).then_inc(dtop_s, 1)

            def gates2(u):
                link = chain(u, GATES1)
                dve.wait_ge(etop_s, u + 1)
                link(v.tensor_scalar(w_2[:, :], etop[:, :], 1.0, None, ALU.add))
                link(v.reciprocal(w_1[:, :], w_2[:, :]))
                link(v.tensor_tensor(w_2[:, :], w_1[:, :], etop[:, :], ALU.mult))
                link(v.tensor_tensor(oh1[:, :, :], oh1[:, :, :], over_experts(w_1), ALU.mult))
                assert link(v.tensor_tensor(oh2[:, :, :], oh2[:, :, :], over_experts(w_2), ALU.mult)) == GATING
                v.tensor_tensor(comb[:, :, :], oh1[:, :, :], oh2[:, :, :], ALU.add).then_inc(comb_s, 1)
                dve.wait_ge(comb_s, 3 * u + 1)
                v.tensor_scalar(combh[:, :, :], comb[:, :, :], 0.5, None, ALU.mult).then_inc(comb_s, 2)

            def expert(st, f, u):
                e, it = divmod(f, 2)
                q, n = f % 2, NF * u + f
                gate, linear, output = expert_banks(u, f)
                if st == "up":
                    dve.wait_ge(m1_mm, 2 * n + 1)
                    if looped(u) or u or f >= 2:
                        dve.wait_ge(act_s, n - 1)
                    v.tensor_scalar(g_sb[:, q, :], gate, b1f[:, e, 0, it:it + 1], LIMIT, ALU.add, ALU.min).then_inc(g_s, 1)
                    dve.wait_ge(m1_mm, 2 * n + 2)
                    v.tensor_scalar(l_sb[:, q, :], linear, b1f[:, e, 1, it:it + 1], 1.0 - LIMIT, ALU.add, ALU.max).then_inc(l_s, 1)
                if st == "down":
                    dve.wait_ge(m2_mm, n + 1)
                    if f == 0:
                        dve.wait_ge(acc_s, 2 * (u + 1))
                    else:
                        dve.wait_ge(m2_ev, 2 * n)
                    for i in range(2):
                        t = 2 * it + i
                        v.scalar_tensor_tensor(acc[:, t, :], output[:, E * i:E * (i + 1)], combh[:, t, e:e + 1], acc[:, t, :],
                                               ALU.mult, ALU.add).then_inc(m2_ev, 1)
                if st == "hidden":
                    dve.wait_ge(th_s, n + 1)
                    v.scalar_tensor_tensor(th_sb[:, q, :], th_sb[:, q, :], 1.0, g_sb[:, q, :], ALU.add, ALU.mult).then_inc(t1_s, 1)
                    dve.wait_ge(t1_s, n + 1)
                    dve.wait_ge(l_s, n + 1)
                    if looped(u) or u or f >= 2:
                        dve.wait_ge(lo_s, n - 1)
                    v.scalar_tensor_tensor(act_sb[:, q, :], l_sb[:, q, :], 1.0 + LIMIT, th_sb[:, q, :],
                                           ALU.min, ALU.mult).then_inc(act_s, 1)
                    if not alone(u):
                        dve.wait_ge(act_s, n + 1)
                        if looped(u) or u or e >= 2:
                            dve.wait_ge(m2_mm, NF * u + 2 * (e - 1))
                        v.tensor_copy(act_hi[:, e % 2, it, :], act_sb[:, q, :]).then_inc(hi_s, 1)

            def final(u, n):
                accv, x1v = (t[:, :, :].rearrange("p t c -> p (t c)") for t in (acc, X1s[:, n]))
                cb, xcv = (t[:, :, :].rearrange("p t c -> p (t c)") for t in (x2b, xc[:, n]))
                dve.wait_ge(m2_ev, 2 * NF * (u + 1))
                v.tensor_copy(cb, accv).then_inc(cb_s, 1)
                dve.wait_ge(cb_s, u + 1)
                v.tensor_tensor(cb, cb, xcv, ALU.add).then_inc(fo_s, 1)
                dve.wait_ge(fo_s, u + 1)
                for hf in range(2):
                    r = slice(C * hf, C * (hf + 1))
                    v.tensor_tensor(accv[:, r], x1v[:, r], cb[:, r], ALU.add).then_inc(x2_s, 1)

            def move_v(b, kt):
                if looped(b) or b >= 0:
                    dve.wait_ge(av_done, NCH * STEPS * b + NCH * STEPS - KT + kt + 1)
                dve.wait_ge(vn_s, 4 * (b + 2))
                v.tensor_copy(V[:, kt, :, 0:HD], Vn[:, kt, :, :]).then_inc(v_s, 1)

            def attend(b, n, s, prep, aside, place=None):
                g, kt = divmod(s, KT)
                first = isinstance(b, int) and b == 0 and n == 0 and g == 0
                if b is not B or g == 0:
                    G = NG * (NCH * b + n) + g - 1
                    if kt == 3 and not first and place in (None, 0):
                        dve.wait_ge(sum_r, 64 * (G + 1))
                        v.reciprocal(rec_c[:, :], sums_c[:, :]).then_inc(rec_s, 1)
                if aside is not None:
                    if n == NCH - 1 and g == NG - 1 and kt and prep:
                        move_v(b, kt - 1)
                    aside(0)
                    aside(1)

            def turn(b):
                move_v(b - 1, KT - 1) if looped(b) or b else [move_v(-1, kt) for kt in range(KT)]
                wait_apart(dve, (flag_s, b + 1))
                flag = dve.value_load(exact_flag[0:1, bass.ds(b, 1)], min_val=0, max_val=1)
                with dve.If(flag > 0):
                    for i in range(128):
                        n, g, j, t = i // 64, i // 16 % NG, i // TC % HG, i % TC
                        wait_apart(dve, (ex_mm, 128 * b + i + 1))
                        h = HG * g + j
                        v.reduce_max(mx[:, TC * n + t, h:h + 1], S[:, i % 2, :], AX_X).then_inc(ex_red, 1)
                    wait_apart(dve, (ex_t, b + 1))
                    if not (isinstance(b, int) and b == 0):
                        wait_apart(dve, (m_w, 16 * b))
                    v.tensor_scalar(Mt[:, 0, :], S[0:H, 0, :], -1.0, None, ALU.mult).then_inc(m_set, 1)
                    wait_apart(dve, (m_set, 2 * b + 1))
                    v.scalar_tensor_tensor(Mt[:, 1, :], S[0:H, 0, :], -1.0, Mt[:, 0, :], ALU.mult, ALU.subtract).then_inc(m_set, 1)
                with dve.If(flag < 1):
                    dve.sem_inc(m_set, 2)
                    dve.sem_inc(ex_red, 128)

            v.memset(half_pow[:, :], -0.5).then_inc(c_set, 1)
            v.memset(OP[:, :], 0.0).then_inc(c_set, 1)
            run(dve, Beside(), stage, attend, lambda: None, turn)


def layouts(np, d):
    f = lambda n: np.asarray(d[n])
    wq, wk, wv, wo = (f(f"L0_attn_W{n}") for n in "qkvo")
    by_channel = lambda w: w.reshape(NG, HG, HD, -1).transpose(0, 2, 1, 3).reshape(E, -1)
    wq, wk, bq, bk = (by_channel(w) for w in (wq, wk, f("L0_attn_bq"), f("L0_attn_bk")))
    w1 = f("L0_ffn_mlp1_weight").reshape(NE, CT, P, 2, CT, P)
    w2 = f("L0_ffn_mlp2_weight").reshape(NE, E, CT, P)
    b1 = f("L0_ffn_mlp1_bias").reshape(NE, CT, P, 2)
    return {
        "x": f("L0_attn_x"),
        "wqk": np.concatenate([wq.T, wk.T], axis=1),
        "bqk": np.concatenate([bq, bk]).reshape(4, P).T,
        "wv": wv.T,
        "bv": f("L0_attn_bv"),
        "wo": wo.T,
        "bo": f("L0_attn_bo"),
        "nw": f("L0_ffn_norm_weight"),
        "gate": f("L0_ffn_gate_weight").T,
        "gate_b": f("L0_ffn_gate_bias"),
        "ones_in": np.ones((MROWS, 2 * HG * L), dtype=f("L0_ffn_gate_weight").dtype),
        "w1": w1.transpose(0, 5, 4, 3, 1, 2).reshape(NE, P, CT, 2 * FI),
        "b1": b1.transpose(2, 0, 3, 1),
        "w2": w2.transpose(0, 3, 2, 1),
        "b2": f("L0_ffn_mlp2_bias"),
    }


def constants(np):
    inv = (1.0 / np.float32(10000.0) ** (np.arange(0, HD, 2, dtype=np.float32) / np.float32(HD))).astype(np.float32)
    ang = (np.arange(L, dtype=np.float32)[:, None] * inv[None, :]).astype(np.float32)
    p = np.arange(P)
    channel, head = p % (HG * HD) // HG, p // (HG * HD) * HG + p % HG
    ang = ang[:, channel // 2].T
    sign = np.where(channel % 2 == 0, -1.0, 1.0).astype(np.float32)[:, None]
    return {
        "rope": np.stack([np.cos(ang), np.sin(ang) * sign]).astype(np.float32),
        "ident_in": np.eye(P, dtype=np.float32),
        "heads_in": (head[:, None] == head[None, :]).astype(np.float32),
        "rank_in": np.arange(NE, 0, -1).astype(np.float32),
    }


def kernel(**inputs):
    import numpy as _np
    import concourse.bacc as _bacc
    from concourse.bass_utils import run_bass_kernel_spmd as _run

    nc = _bacc.Bacc("TRN2", target_bir_lowering=False, num_devices=1)
    arrays, args = {}, {}
    for name, a in {**layouts(_np, inputs), **constants(_np)}.items():
        a = _np.ascontiguousarray(a)
        arrays[f"in_{name}"] = a
        args[name] = nc.dram_tensor(f"in_{name}", a.shape, mybir.dt.from_np(a.dtype), kind="ExternalInput").ap()
    args["out"] = nc.dram_tensor("out_0", (B, L, E), FP32, kind="ExternalOutput").ap()
    block_kernel(nc, **args)
    r = _run(nc, [arrays], core_ids=[0])
    return r.results[0]["out_0"]
```
